# Optimizing a Trainium2 kernel written in Bass

```python
import numpy as np
import jax
import jax.numpy as jnp

def _softmax(x, axis=-1):
    return jax.nn.softmax(x, axis=axis)

def _gelu(x):
    return jax.nn.gelu(x, approximate=True)

def _silu(x):
    return jax.nn.silu(x)

def _sigmoid(x):
    return jax.nn.sigmoid(x)

def _layernorm(x, axis=-1, eps=1e-05):
    m = jnp.mean(x, axis=axis, keepdims=True)
    v = jnp.var(x, axis=axis, keepdims=True)
    return (x - m) / jnp.sqrt(v + eps)

def _scatter_add(tgt, idx, src, axis=0):
    return tgt.at[idx].add(src)

def _segment_sum(src, seg, n):
    return jax.ops.segment_sum(src, seg, n)
kernel_name = 'mk_adaln_d1_jaxref_r8_563a82'

def setup_inputs(seed: int=0):
    np.random.seed(seed)
    _w = jnp.asarray

    def _L0_attn_setup():
        import jax, jax.numpy as jnp
        import numpy as np
        D_HEAD = 64
        MASK_FILL = -1000000.0
        key = jax.random.key(seed)
        ks = jax.random.split(key, 5)
        batch, seq, d_model, n_heads, d_head = (4, 256, 128, 16, D_HEAD)
        bound_qkv = float(np.sqrt(6.0 / (d_model + n_heads * d_head)))
        bound_out = float(np.sqrt(6.0 / (d_head + n_heads * d_model)))
        return {'resid': jax.random.normal(ks[0], (batch, seq, d_model), dtype=jnp.float32), 'W_Q': jax.random.uniform(ks[1], (d_model, n_heads, d_head), jnp.float32, -bound_qkv, bound_qkv), 'W_K': jax.random.uniform(ks[2], (d_model, n_heads, d_head), jnp.float32, -bound_qkv, bound_qkv), 'W_V': jax.random.uniform(ks[3], (d_model, n_heads, d_head), jnp.float32, -bound_qkv, bound_qkv), 'W_out': jax.random.uniform(ks[4], (d_head, n_heads, d_model), jnp.float32, -bound_out, bound_out), 'b_out': jnp.zeros((d_model,), dtype=jnp.float32)}
    _L0_attn_in = _L0_attn_setup()

    def _L0_ffn_setup():
        import jax, jax.numpy as jnp
        import numpy as np
        from jax import lax
        D = 128
        H = 512
        E = 8
        TOPK = 2
        key = jax.random.key(seed)
        ks = jax.random.split(key, 7)
        s = 0.02
        return {'x': jax.random.normal(ks[0], (2, 256, D), dtype=jnp.float32), 'W1': jax.random.normal(ks[1], (E, D, H), dtype=jnp.float32) * s, 'b1': jnp.zeros((E, H), dtype=jnp.float32), 'W2': jax.random.normal(ks[2], (E, H, D), dtype=jnp.float32) * s, 'b2': jnp.zeros((E, D), dtype=jnp.float32), 'Wr': jax.random.normal(ks[3], (D, E), dtype=jnp.float32) * s, 'br': jnp.zeros((E,), dtype=jnp.float32)}
    _L0_ffn_in = _L0_ffn_setup()
    _L0_c = _w((lambda *s: np.random.randn(*s).astype(np.float32) * 0.05)(16, 128))
    _L0_wmod = _w((lambda *s: np.random.randn(*s).astype(np.float32) * 0.05)(128, 6 * 128) * 128 ** (-0.5))
    _d = {'L0_attn_resid': _L0_attn_in['resid'], 'L0_attn_W_Q': _L0_attn_in['W_Q'], 'L0_attn_W_K': _L0_attn_in['W_K'], 'L0_attn_W_V': _L0_attn_in['W_V'], 'L0_attn_W_out': _L0_attn_in['W_out'], 'L0_attn_b_out': _L0_attn_in['b_out'], 'L0_ffn_W1': _L0_ffn_in['W1'], 'L0_ffn_b1': _L0_ffn_in['b1'], 'L0_ffn_W2': _L0_ffn_in['W2'], 'L0_ffn_b2': _L0_ffn_in['b2'], 'L0_ffn_Wr': _L0_ffn_in['Wr'], 'L0_ffn_br': _L0_ffn_in['br'], 'L0_c': _L0_c, 'L0_wmod': _L0_wmod}
    _x0 = _d['L0_attn_resid']
    _d['L0_attn_resid'] = jax.random.normal(jax.random.fold_in(jax.random.key(seed), 1), (16, 512, 128), dtype=_x0.dtype)
    del _x0
    return _d

def reference(L0_attn_resid, L0_attn_W_Q, L0_attn_W_K, L0_attn_W_V, L0_attn_W_out, L0_attn_b_out, L0_ffn_W1, L0_ffn_b1, L0_ffn_W2, L0_ffn_b2, L0_ffn_Wr, L0_ffn_br, L0_c, L0_wmod):

    def _L0_attn_ref(resid, W_Q, W_K, W_V, W_out, b_out):
        import jax, jax.numpy as jnp
        import numpy as np
        D_HEAD = 64
        MASK_FILL = -1000000.0
        seq = resid.shape[1]
        d_head = W_Q.shape[-1]
        q = jnp.einsum('bsd,dhk->bshk', resid, W_Q)
        k = jnp.einsum('bsd,dhk->bshk', resid, W_K)
        v = jnp.einsum('bsd,dhk->bshk', resid, W_V)
        scores = jnp.einsum('bqhk,bkhd->bhqd', q, k.astype(q.dtype)) if False else jnp.einsum('bqhc,bshc->bhqs', q, k)
        scores = scores / jnp.sqrt(jnp.asarray(d_head, dtype=scores.dtype))
        causal_mask = jnp.triu(jnp.ones((seq, seq), dtype=bool), k=1)
        scores = jnp.where(causal_mask, MASK_FILL, scores)
        probs = jax.nn.softmax(scores, axis=-1)
        z = jnp.einsum('bhqs,bshc->bqhc', probs, v)
        out = jnp.einsum('bqhc,chd->bqd', z, W_out) + b_out
        return out

    def _L0_ffn_ref(x, W1, b1, W2, b2, Wr, br):
        import jax, jax.numpy as jnp
        import numpy as np
        from jax import lax
        D = 128
        H = 512
        E = 8
        TOPK = 2
        B, S, _ = x.shape
        xf = x.reshape(-1, D)
        logits = xf @ Wr + br
        topv, _ = lax.top_k(logits, TOPK)
        thresh = topv[:, TOPK - 1:TOPK]
        masked = jnp.where(logits >= thresh, logits, -jnp.inf)
        weights = jax.nn.softmax(masked, axis=-1)
        h = jax.nn.gelu(jnp.einsum('td,edh->eth', xf, W1) + b1[:, None, :], approximate=False)
        expert_out = jnp.einsum('eth,ehd->etd', h, W2) + b2[:, None, :]
        out = jnp.einsum('etd,te->td', expert_out, weights)
        return out.reshape(B, S, D)
    x = L0_attn_resid
    mod = (_silu(L0_c) @ L0_wmod).reshape(L0_c.shape[0], 6, 1, -1)
    sa, ca, ga, sb, cb, gb = (mod[:, 0], mod[:, 1], mod[:, 2], mod[:, 3], mod[:, 4], mod[:, 5])
    ga = (2 * (ga >= 0) - 1) * jnp.maximum(jnp.abs(ga), 0.25)
    gb = (2 * (gb >= 0) - 1) * jnp.maximum(jnp.abs(gb), 0.25)
    h = _layernorm(x, axis=-1) * (1 + ca) + sa
    x = x + ga * _L0_attn_ref(h, L0_attn_W_Q, L0_attn_W_K, L0_attn_W_V, L0_attn_W_out, L0_attn_b_out)
    h = _layernorm(x, axis=-1) * (1 + cb) + sb
    x = x + gb * _L0_ffn_ref(h, L0_ffn_W1, L0_ffn_b1, L0_ffn_W2, L0_ffn_b2, L0_ffn_Wr, L0_ffn_br)
    return x

_drawn_inputs = setup_inputs


def setup_inputs(seed=0):
    import zlib

    import numpy as np

    out = dict(_drawn_inputs(seed))
    spreads = {'L0_attn_b_out': (0.0, 0.338),
     'L0_ffn_b1': (0.0, 0.8),
     'L0_ffn_b2': (0.0, 0.487),
     'L0_ffn_br': (0.0, 0.46)}
    factors = {'L0_attn_W_Q': 8.0,
     'L0_attn_W_K': 8.0,
     'L0_attn_W_V': 4.134,
     'L0_attn_W_out': 4.081,
     'L0_ffn_W1': 5.97,
     'L0_ffn_W2': 5.39,
     'L0_ffn_Wr': 3.655}
    for name, (base, spread) in spreads.items():
        noise = np.random.default_rng([zlib.crc32(name.encode()), seed]).standard_normal(out[name].shape)
        drawn = base * np.exp(spread * noise) if base else spread * noise
        out[name] = jnp.asarray(drawn.astype(out[name].dtype))
    for name, factor in factors.items():
        out[name] = (out[name] * factor).astype(out[name].dtype)
    return out
```

```python
from contextlib import ExitStack

import concourse.bass as bass
from concourse import mybir

F32 = mybir.dt.float32
F32R = mybir.dt.float32r
ALU = mybir.AluOpType
ACT = mybir.ActivationFunctionType
AX = mybir.AxisListType
ds = bass.ds

P = 128
EPS = 1e-5
NEG = -1e30
BIG = 3e38
GATE_MIN = 0.25

ROW_ORDER = [3, 2, 0, 1]
UNITS = [[3], [2, 0], [1]]
UNIT_END = [1, 3, 4]
ROW_AT = {3: 0, 2: 512, 0: 896, 1: 1024}
ROW_IN_BANK = {3: 0, 2: 0, 0: 384, 1: 0}
HEAD_COLS = 1280
KEY_AT = {0: 0, 1: 512, 3: 896, 2: 1024}


def adaln_moe_kernel(nc, resid, W_Q, W_K, W_V, W_out, b_out, W1, b1, W2, b2, Wr, br, c_in, wmod, out):
    B, S, D = resid.shape
    NH, DH = W_Q.shape[1], W_Q.shape[2]
    E, _, H = W1.shape
    NT = S // P
    NP = NH // 2
    HC = H // P
    QK = NH * DH
    SCALE = float(DH) ** -0.5
    assert D == P and S == 512 and DH == 64 and NP == 8 and E == 8 and HC == 4 and B >= 3

    gates_dram = nc.dram_tensor("gates_dram", (B, 2 * D), F32, kind="Internal").ap()

    with ExitStack() as ctx:
        def sb(name, shape, dt=F32, at=ctx):
            return at.enter_context(nc.sbuf_tensor(name, shape, dt))

        def sem(name):
            return ctx.enter_context(nc.semaphore(name))

        banks = ctx.enter_context(nc.psum_tensor("banks", [P, 8, 512], F32))
        q_bank, k_bank = banks[:, 0, :], banks[:, 1, :]
        s_banks = [banks[:, 2 + i, :] for i in range(3)]
        t_banks = [banks[:, 5 + i, :] for i in range(2)]
        g_bank = banks[:, 7, :]

        x_all = sb("x_all", [P, B * NT, D])
        ident = sb("ident", [P, P])
        mod_cols = sb("mod_cols", [P, 6, B])
        gate_a = sb("gate_a", [P, B, D])
        gate_b = sb("gate_b", [P, B, D])
        neg_half = sb("neg_half", [P, NT])
        b1_cols = sb("b1_cols", [P, E * HC])
        b2_rows = sb("b2_rows", [E, D])
        wr_sb = sb("wr_sb", [D, E])
        br_b = sb("br_b", [P, E])
        stats = sb("stats", [P, NT, 6])
        meanvar = sb("meanvar", [P, NT, 2])
        var_eps = sb("var_eps", [P, NT])
        rstd = sb("rstd", [P, NT])
        xn = sb("xn", [P, NT, D])
        hf = sb("hf", [P, S])

        def pair(per, b, p):
            return per * NP * b + per * p

        def wait_alone(engine, semaphore, count):
            engine.wait_ge(semaphore, count)
            engine.nop(nofuse=True)

        def batches(engine, body):
            body(0, True, False)
            with engine.Fori(1, B - 1) as b:
                body(b, False, False)
            body(B - 1, False, True)

        def before(b, p):
            return (b, p - 1) if p > 0 else (b - 1, NP - 1)

        def after(b, p):
            return (b, p + 1) if p < NP - 1 else (b + 1, 0)

        x_in = sem("x_in")

        with ExitStack() as pa:
            def sa(name, shape, dt=F32):
                return sb(name, shape, dt, pa)

            wq = [sa("wq_hi", [P, QK], F32R), sa("wq_lo", [P, QK], F32R)]
            wk = [sa("wk_hi", [P, QK], F32R), sa("wk_lo", [P, QK], F32R)]
            wv = [sa("wv_hi", [P, QK], F32R), sa("wv_lo", [P, QK], F32R)]
            wo = sa("wo", [P, NP, D])
            bo_b = sa("bo_b", [P, D])
            q_split = sa("q_split", [P, 2, 2, S], F32R)
            k_hi2 = sa("k_hi2", [P, 2, 2, S], F32R)
            k_rest = sa("k_rest", [P, 2, 2, S], F32R)
            masked = sa("masked", [P, 2, HEAD_COLS])
            probs = sa("probs", [P, 2, HEAD_COLS])
            probs_T = sa("probs_T", [P, 2, HEAD_COLS])
            v_sb = sa("v_sb", [P, NT, QK])
            z_T = sa("z_T", [P, NP, S])
            h_hi = sa("h_hi", [P, S], F32R)
            h_lo = sa("h_lo", [P, S], F32R)
            attn = sa("attn", [P, NT, D])
            mask_w = sa("mask_w", [P, 512])
            neg_max = sa("neg_max", [P, 8])
            denom = sa("denom", [P, 8])
            rdenom = sa("rdenom", [P, 8])

            with ExitStack() as ps:
                raw_w = [v_sb[:, i, :] for i in range(3)]
                zv = z_T[:, :, :].rearrange("p a n -> p (a n)")
                wmod_sb = zv[:, 0:6 * D]
                c_rows = zv[0:B, 1024:1024 + D]
                b1_rows = zv[0:E * HC, 1152:1152 + P]
                c_cols = zv[:, 1280:1280 + B]
                e_c = zv[:, 1312:1312 + B]
                e1_c = zv[:, 1344:1344 + B]
                sig_c = zv[:, 1376:1376 + B]
                silu_c = zv[:, 1408:1408 + B]
                g_raw = zv[0:B, 1536:1536 + 2 * D]
                g_sign = zv[0:B, 2048:2048 + 2 * D]
                g_mag = zv[0:B, 2560:2560 + 2 * D]
                g_out = zv[0:B, 3072:3072 + 2 * D]

                load_rows = sem("load_rows")
                load_w = sem("load_w")
                load_mod = sem("load_mod")
                load_kept = sem("load_kept")
                pool_zero = sem("pool_zero")
                pool_const = sem("pool_const")
                cols_ps = sem("cols_ps")
                exp_c = sem("exp_c")
                dve_chain = sem("dve_chain")
                cols_ok = sem("cols_ok")
                silu_ok = sem("silu_ok")
                mod_ps = sem("mod_ps")
                gates_ok = sem("gates_ok")
                gates_out = sem("gates_out")
                gates_in = sem("gates_in")

                with nc.Block() as block:
                    @block.sync
                    def _(sp):
                        sp.dma_start(c_rows, c_in).then_inc(load_rows, 16)
                        sp.dma_start(b1_rows, b1.rearrange("e (c p) -> (e c) p", p=P)).then_inc(load_rows, 16)
                        sp.dma_start(wmod_sb, wmod).then_inc(load_mod, 16)
                        for dst, src in zip(raw_w, (W_Q, W_K, W_V)):
                            sp.dma_start(dst, src.rearrange("d h c -> d (h c)")).then_inc(load_w, 16)
                        sp.dma_start(x_all[:, 0:NT, :], resid[0].rearrange("(t p) d -> p t d", p=P)).then_inc(x_in, 16)
                        sp.wait_ge(gates_ok, 1)
                        sp.dma_start(gates_dram, g_out).then_inc(gates_out, 16)
                        sp.wait_ge(gates_out, 16)
                        gv = gates_dram.rearrange("b (g d) -> g b d", g=2)
                        for g, dst in enumerate((gate_a, gate_b)):
                            sp.dma_start(dst[:, :, :], gv[g].partition_broadcast(P)).then_inc(gates_in, 16)
                        sp.wait_ge(gates_in, 32)

                    @block.gpsimd
                    def _(pool):
                        pool.memset(ident[:, :], 0.0).then_inc(pool_zero, 1)
                        pool.memset(mask_w[:, :], 0.0).then_inc(pool_zero, 1)
                        pool.memset(neg_half[:, :], -0.5).then_inc(pool_const, 1)
                        pool.wait_ge(pool_zero, 2)
                        pool.affine_select(out=ident[:, :], in_=ident[:, :], compare_op=ALU.not_equal, fill=1.0,
                                           base=0, pattern=[[-1, P]], channel_multiplier=1).then_inc(pool_const, 1)
                        pool.affine_select(out=mask_w[:, 384:512], in_=mask_w[:, 384:512], compare_op=ALU.is_ge,
                                           fill=NEG, base=0, pattern=[[-1, P]], channel_multiplier=1)\
                            .then_inc(pool_const, 1)
                        pool.dma_start(bo_b[:, :], b_out.partition_broadcast(P)).then_inc(load_kept, 16)
                        pool.dma_start(br_b[:, :], br.partition_broadcast(P)).then_inc(load_kept, 16)
                        pool.dma_start(b2_rows[:, :], b2).then_inc(load_kept, 16)
                        pool.dma_start(wr_sb[:, :], Wr).then_inc(load_kept, 16)
                        wo_v = W_out.rearrange("c (n two) d -> two c n d", two=2)
                        for half in range(2):
                            pool.dma_start(wo[half * DH:(half + 1) * DH, :, :], wo_v[half]).then_inc(load_kept, 16)
                        pool.wait_ge(load_kept, 96)

                    @block.tensor
                    def _(pe):
                        pe.wait_ge(pool_const, 3)
                        pe.wait_ge(load_rows, 32)
                        pe.transpose(g_bank[:, 0:B], c_rows, ident[0:B, 0:B])
                        pe.transpose(g_bank[:, B:B + E * HC], b1_rows, ident[0:E * HC, 0:E * HC]).then_inc(cols_ps, 1)
                        pe.wait_ge(silu_ok, 1)
                        pe.wait_ge(load_mod, 16)
                        for j in range(6):
                            pe.matmul(s_banks[0][:, j * B:(j + 1) * B], wmod_sb[:, j * D:(j + 1) * D], silu_c,
                                      start=True, stop=True)
                        for g, j in enumerate((2, 5)):
                            mm = pe.matmul(s_banks[1][0:B, g * D:(g + 1) * D], silu_c, wmod_sb[:, j * D:(j + 1) * D],
                                           start=True, stop=True)
                        mm.then_inc(mod_ps, 1)

                    @block.scalar
                    def _(act):
                        act.wait_ge(cols_ok, 2)
                        act.activation(e_c, c_cols, ACT.Exp, scale=-1.0).then_inc(exp_c, 1)

                    @block.vector
                    def _(dve):
                        done = [0]

                        def link(ins):
                            done[0] += 1
                            ins.then_inc(dve_chain, 1)
                            dve.wait_ge(dve_chain, done[0])

                        dve.wait_ge(cols_ps, 1)
                        dve.tensor_copy(c_cols, g_bank[:, 0:B]).then_inc(cols_ok, 1)
                        dve.tensor_copy(b1_cols[:, :], g_bank[:, B:B + E * HC]).then_inc(cols_ok, 1)
                        dve.wait_ge(exp_c, 1)
                        link(dve.tensor_scalar(e1_c, e_c, 1.0, None, ALU.add))
                        link(dve.reciprocal(sig_c, e1_c))
                        dve.tensor_tensor(silu_c, c_cols, sig_c, ALU.mult).then_inc(silu_ok, 1)
                        dve.wait_ge(mod_ps, 1)
                        link(dve.tensor_copy(mod_cols[:, :, :].rearrange("p j b -> p (j b)"), s_banks[0][:, 0:6 * B]))
                        for j in (1, 4):
                            link(dve.tensor_scalar(mod_cols[:, j, :], mod_cols[:, j, :], 1.0, None, ALU.add))
                        link(dve.tensor_copy(g_raw, s_banks[1][0:B, 0:2 * D]))
                        link(dve.tensor_scalar(g_sign, g_raw, 0.0, 2.0, ALU.is_ge, ALU.mult))
                        link(dve.tensor_scalar(g_sign, g_sign, 1.0, None, ALU.subtract))
                        link(dve.tensor_tensor(g_mag, g_raw, g_sign, ALU.mult))
                        dve.scalar_tensor_tensor(out=g_out, in0=g_mag, scalar=GATE_MIN, in1=g_sign,
                                                 op0=ALU.max, op1=ALU.mult).then_inc(gates_ok, 1)
                        link(dve.memset(k_rest[:, :, :, :].rearrange("p a b n -> p (a b n)").bitcast(F32), 0.0))
                        dve.wait_ge(load_w, 48)
                        for (hi, lo), raw in zip((wq, wk, wv), raw_w):
                            link(dve.tensor_copy(hi[:, :], raw))
                            link(dve.tensor_tensor(lo[:, :], raw, hi[:, :].bitcast(F32), ALU.subtract))

            qk_ps = sem("qk_ps")
            s_ps = sem("s_ps")
            t_ps = sem("t_ps")
            z_ps = sem("z_ps")
            v_ps = sem("v_ps")
            lnT_ps = sem("lnT_ps")
            o_ps = sem("o_ps")
            q_hi = sem("q_hi")
            k_hi = sem("k_hi")
            t_act = sem("t_act")
            p_exp = sem("p_exp")
            v_act = sem("v_act")
            h_full = sem("h_full")
            q_lo = sem("q_lo")
            k_lo = sem("k_lo")
            t_dve = sem("t_dve")
            s_masked = sem("s_masked")
            rden = sem("rden")
            z_done = sem("z_done")
            ln_stat = sem("ln_stat")
            ln_mv = sem("ln_mv")
            ln_xn = sem("ln_xn")
            h_rounded = sem("h_rounded")
            h_rest = sem("h_rest")
            o_biased = sem("o_biased")
            o_gated = sem("o_gated")
            x_mid = sem("x_mid")
            p_norm = sem("p_norm")
            ln_eps = sem("ln_eps")
            ln_rstd = sem("ln_rstd")
            k_dup = [sem("k_dup0"), sem("k_dup1")]

            with nc.Block() as block:
                @block.sync
                def _(sp):
                    def dup(b, p):
                        for h in range(2):
                            src, dst = (0, DH) if h == 0 else (DH, 0)
                            sp.wait_ge(k_hi, pair(2, b, p) + h + 1)
                            sp.dma_start(k_hi2[dst:dst + DH, p % 2, h, :].bitcast(F32),
                                         k_hi2[src:src + DH, p % 2, h, :].bitcast(F32)).then_inc(k_dup[p % 2], 16)

                    def body(b, first, last):
                        if first:
                            dup(0, 0)
                        for p in range(NP):
                            if p == 0 and not last:
                                sp.wait_ge(x_in, 16 * b + 16)
                                sp.dma_start(x_all[:, ds((b + 1) * NT, NT), :],
                                             resid[ds(b + 1, 1)].rearrange("b (t p) d -> p (b t) d", p=P))\
                                    .then_inc(x_in, 16)
                            if not (last and p == NP - 1):
                                dup(*after(b, p))

                    batches(sp, body)

                @block.gpsimd
                def _(pool):
                    def inv_std(b):
                        wait_alone(pool, ln_mv, NT * b + NT)
                        pool.tensor_scalar(var_eps[:, :], meanvar[:, :, 1], EPS, 1.0, ALU.add, ALU.mult)\
                            .then_inc(ln_eps, 1)
                        pool.wait_ge(ln_eps, b + 1)
                        pool.tensor_tensor(rstd[:, :], var_eps[:, :], neg_half[:, :], ALU.pow).then_inc(ln_rstd, 1)

                    inv_std(0)

                    def body(b, first, last):
                        for p in range(NP):
                            if p == 4 and not last:
                                inv_std(b + 1)
                            for h in range(2):
                                wait_alone(pool, rden, pair(2, b, p) + h + 1)
                                for r in ROW_ORDER:
                                    at, n = ROW_AT[r], (r + 1) * P
                                    pool.tensor_scalar(probs[:, h, at:at + n], probs[:, h, at:at + n],
                                                       rdenom[:, 4 * h + r:4 * h + r + 1], 1.0, ALU.mult, ALU.mult)\
                                        .then_inc(p_norm, 1)

                    batches(pool, body)

                @block.tensor
                def _(pe):
                    def split_product(ps, a, b):
                        pe.matmul(ps, a[0], b[0], start=True, stop=False)
                        pe.matmul(ps, a[1], b[0], start=False, stop=False)
                        return pe.matmul(ps, a[0], b[1], start=False, stop=True)

                    h_cols = (h_hi[:, :], h_lo[:, :])

                    def project(b, p, v_before):
                        pe.wait_ge(h_rest, b + 1)
                        for w, bank, read in ((wq, q_bank, q_lo), (wk, k_bank, k_lo)):
                            if v_before is not None:
                                pe.wait_ge(v_act, 8 * v_before + 8)
                            elif not isinstance(b, int) or b > 0 or p > 0:
                                pe.wait_ge(read, pair(2, b, p))
                            cols = slice(p * P, (p + 1) * P)
                            split_product(bank, (w[0][:, cols], w[1][:, cols]), h_cols).then_inc(qk_ps, 1)

                    def h_transposes(b):
                        pe.wait_ge(ln_xn, NT * b + NT)
                        for t in range(NT):
                            mm = pe.transpose(g_bank[:, t * P:(t + 1) * P], xn[:, t, :], ident[:, :])
                        mm.then_inc(lnT_ps, 1)

                    def scores(b, p, first):
                        pe.wait_ge(q_lo, pair(2, b, p) + 2)
                        pe.wait_ge(k_lo, pair(2, b, p) + 2)
                        pe.wait_ge(k_dup[p % 2], 128 * b + 32 * (p // 2) + 32)
                        for h in range(2):
                            for u, rows in enumerate(UNITS):
                                if h == 1:
                                    pe.wait_ge(s_masked, pair(8, b, p) + UNIT_END[u])
                                elif not first:
                                    pe.wait_ge(s_masked, pair(8, b, p) - 4 + UNIT_END[u])
                                for r in rows:
                                    n = (r + 1) * P
                                    at = ROW_IN_BANK[r]
                                    ps = s_banks[u][:, at:at + n]
                                    q = q_split[:, p % 2, h, r * P:(r + 1) * P]
                                    pe.matmul(ps, q, k_hi2[:, p % 2, h, 0:n], start=True, stop=False)
                                    mm = pe.matmul(ps, q, k_rest[:, p % 2, h, 0:n], start=False, stop=True)
                                mm.then_inc(s_ps, 1)

                    def transposes(b, p, first):
                        units = [[(0, 0, r, r * P) for r in range(4)],
                                 [(0, 1, r, (r - 1) * P) for r in range(1, 4)] + [(0, 3, 3, 384)],
                                 [(1, 0, r, r * P) for r in range(4)],
                                 [(1, 1, r, (r - 1) * P) for r in range(1, 4)] + [(1, 3, 3, 384)],
                                 [(h, 2, r, 256 * h + (r - 2) * P) for h in range(2) for r in (2, 3)]]
                        for u, blocks in enumerate(units):
                            if u == 0:
                                pe.wait_ge(p_norm, pair(8, b, p) + 4)
                            if u == 2:
                                pe.wait_ge(p_norm, pair(8, b, p) + 8)
                            if u == 0 and not first:
                                pe.wait_ge(t_act, pair(2, b, p))
                            if u == 1 and not first:
                                pe.wait_ge(t_dve, pair(3, b, p))
                            if u == 2:
                                pe.wait_ge(t_dve, pair(3, b, p) + 1)
                            if u == 3:
                                pe.wait_ge(t_act, pair(2, b, p) + 1)
                            if u == 4:
                                pe.wait_ge(t_dve, pair(3, b, p) + 2)
                            bank = t_banks[(5 * p + u) % 2]
                            for h, c, r, at in blocks:
                                src = ROW_AT[r] + c * P
                                mm = pe.transpose(bank[:, at:at + P], probs[:, h, src:src + P], ident[:, :])
                            mm.then_inc(t_ps, 1)

                    def weigh_values(b, p, g_free):
                        pe.wait_ge(t_dve, pair(3, b, p) + 3)
                        pe.wait_ge(t_act, pair(2, b, p) + 2)
                        pe.wait_ge(v_act, 8 * b + 8)
                        for s, n in g_free:
                            pe.wait_ge(s, n)
                        for c in range(NT):
                            for h in range(2):
                                n = S - c * P
                                hc = (2 * p + h) * DH
                                mm = pe.matmul(g_bank[h * DH:(h + 1) * DH, c * P:S], v_sb[:, c, hc:hc + DH],
                                               probs_T[:, h, KEY_AT[c]:KEY_AT[c] + n], start=(c == 0), stop=(c == NT - 1))
                        mm.then_inc(z_ps, 1)

                    def values(b):
                        for i in range(8):
                            t, half = i // 2, i % 2
                            if i == 0:
                                pe.wait_ge(q_lo, pair(2, b, 2))
                                pe.wait_ge(k_lo, pair(2, b, 2))
                            if i >= 2:
                                pe.wait_ge(v_act, 8 * b + i - 1)
                            toks, cols = slice(t * P, (t + 1) * P), slice(half * 512, half * 512 + 512)
                            split_product((q_bank, k_bank)[i % 2], (h_hi[:, toks], h_lo[:, toks]),
                                          (wv[0][:, cols], wv[1][:, cols])).then_inc(v_ps, 1)

                    def project_out(b):
                        pe.wait_ge(z_done, pair(1, b, NP))
                        for t in range(NT):
                            for p in range(NP):
                                mm = pe.matmul(g_bank[:, t * P:(t + 1) * P], z_T[:, p, t * P:(t + 1) * P], wo[:, p, :],
                                               start=(p == 0), stop=(p == NP - 1))
                        mm.then_inc(o_ps, 1)

                    def body(b, first, last):
                        if first:
                            h_transposes(0)
                            project(0, 0, None)
                        for p in range(NP):
                            begin = first and p == 0
                            if not (last and p == NP - 1):
                                project(*after(b, p), b if p == 1 else None)
                            if p == 6 and not last:
                                pe.wait_ge(z_done, pair(1, b, p) - 1)
                                h_transposes(b + 1)
                            if not begin:
                                transposes(*before(b, p), first and p == 1)
                            scores(b, p, begin)
                            if p == 1 and not first:
                                project_out(b - 1)
                            if not begin:
                                if p == 6 and not last:
                                    g_free = [(h_full, b + 2)]
                                elif p == 1:
                                    g_free = [] if first else [(o_biased, b)]
                                else:
                                    g_free = [(z_done, pair(1, *before(b, p)))]
                                if first and p == 1:
                                    g_free = [(h_full, 1)]
                                weigh_values(*before(b, p), g_free)
                            if p == 0:
                                values(b)

                    batches(pe, body)
                    transposes(B - 1, NP - 1, False)
                    weigh_values(B - 1, NP - 1, [(z_done, pair(1, B - 1, NP - 1))])
                    project_out(B - 1)

                @block.scalar
                def _(act):
                    def h_evac(b):
                        act.wait_ge(lnT_ps, b + 1)
                        if not isinstance(b, int) or b > 0:
                            act.wait_ge(h_rest, b)
                        act.activation(hf[:, :], g_bank, ACT.Identity, bias=mod_cols[:, 0, ds(b, 1)],
                                       scale=mod_cols[:, 1, ds(b, 1)]).then_inc(h_full, 1)

                    def round_qk(b, p, reused):
                        for n, (dst, bank, done) in enumerate(((q_split, q_bank, q_hi), (k_hi2, k_bank, k_hi))):
                            act.wait_ge(qk_ps, pair(2, b, p) + n + 1)
                            if reused and n == 0:
                                act.wait_ge(s_ps, pair(6, b, p) - 6)
                            for h in range(2):
                                half = slice(h * DH, (h + 1) * DH)
                                act.activation(dst[half, p % 2, h, :], bank[half, :], ACT.Copy).then_inc(done, 1)

                    def evac_T(b, p, first):
                        for n, u in enumerate((1, 3)):
                            act.wait_ge(t_ps, pair(5, b, p) + u + 1)
                            if not first:
                                act.wait_ge(z_ps, pair(1, b, p))
                            act.activation(probs_T[:, u // 2, 512:1024], t_banks[(5 * p + u) % 2], ACT.Copy)\
                                .then_inc(t_act, 1)

                    h_evac(0)
                    round_qk(0, 0, False)

                    def body(b, first, last):
                        for p in range(NP):
                            begin = first and p == 0
                            if not (last and p == NP - 1):
                                round_qk(*after(b, p), not begin)
                            if p == 6 and not last:
                                h_evac(b + 1)
                            if not begin:
                                evac_T(*before(b, p), first and p == 1)
                            for i in range(8):
                                h, r = i // 4, ROW_ORDER[i % 4]
                                at, n = ROW_AT[r], (r + 1) * P
                                act.wait_ge(s_masked, pair(8, b, p) + i + 1)
                                if i == 0 and not begin:
                                    act.wait_ge(t_ps, pair(5, b, p))
                                act.activation(probs[:, h, at:at + n], masked[:, h, at:at + n], ACT.Exp,
                                               bias=neg_max[:, 4 * h + r:4 * h + r + 1], scale=-1.0,
                                               accum_out=denom[:, 4 * h + r:4 * h + r + 1]).then_inc(p_exp, 1)
                            if p == 0:
                                for i in range(8):
                                    t, half = i // 2, i % 2
                                    act.wait_ge(v_ps, 8 * b + i + 1)
                                    act.activation(v_sb[:, t, half * 512:(half + 1) * 512],
                                                   (q_bank, k_bank)[i % 2], ACT.Copy).then_inc(v_act, 1)

                    batches(act, body)
                    evac_T(B - 1, NP - 1, False)

                @block.vector
                def _(dve):
                    def ln_stats(b):
                        dve.wait_ge(x_in, 16 * b + 16)
                        for t in range(NT):
                            dve.bn_stats(stats[:, t, :], x_all[:, ds(b * NT + t, 1), :].rearrange("p a d -> p (a d)"))\
                                .then_inc(ln_stat, 1)
                        for t in range(NT):
                            wait_alone(dve, ln_stat, NT * b + t + 1)
                            dve.bn_aggr(meanvar[:, t, :], stats[:, t, :]).then_inc(ln_mv, 1)

                    def ln_apply(b):
                        dve.wait_ge(ln_rstd, b + 1)
                        if not isinstance(b, int) or b > 0:
                            dve.wait_ge(lnT_ps, b)
                        for t in range(NT):
                            dve.tensor_scalar(xn[:, t, :], x_all[:, ds(b * NT + t, 1), :].rearrange("p a d -> p (a d)"),
                                              meanvar[:, t, 0:1], rstd[:, t:t + 1], ALU.subtract, ALU.mult)\
                                .then_inc(ln_xn, 1)

                    def split_h(b):
                        dve.wait_ge(h_full, b + 1)
                        if not isinstance(b, int) or b > 0:
                            dve.wait_ge(qk_ps, pair(2, b, 0))
                        dve.tensor_copy(h_hi[:, :], hf[:, :]).then_inc(h_rounded, 1)
                        dve.wait_ge(h_rounded, b + 1)
                        dve.tensor_tensor(h_lo[:, :], hf[:, :], h_hi[:, :].bitcast(F32), ALU.subtract).then_inc(h_rest, 1)

                    def rest_qk(b, p):
                        for h in range(2):
                            own, other = slice(h * DH, (h + 1) * DH), slice((1 - h) * DH, (2 - h) * DH)
                            dve.wait_ge(q_hi, pair(2, b, p) + h + 1)
                            dve.tensor_tensor(q_split[other, p % 2, h, :], q_bank[own, :],
                                              q_split[own, p % 2, h, :].bitcast(F32), ALU.subtract).then_inc(q_lo, 1)
                        for h in range(2):
                            own = slice(h * DH, (h + 1) * DH)
                            dve.wait_ge(k_hi, pair(2, b, p) + h + 1)
                            dve.tensor_tensor(k_rest[own, p % 2, h, :], k_bank[own, :],
                                              k_hi2[own, p % 2, h, :].bitcast(F32), ALU.subtract).then_inc(k_lo, 1)

                    def evac_T(b, p, first):
                        for u in (0, 2, 4):
                            dve.wait_ge(t_ps, pair(5, b, p) + u + 1)
                            if not first:
                                dve.wait_ge(z_ps, pair(1, b, p))
                            bank = t_banks[(5 * p + u) % 2]
                            if u < 4:
                                dst, src = probs_T[:, u // 2, 0:512], bank
                            else:
                                dst, src = probs_T[:, :, 1024:1280], bank.rearrange("p (h n) -> p h n", h=2)
                            dve.tensor_copy(dst, src).then_inc(t_dve, 1)

                    def mask_and_max(b, p, begin):
                        for h in range(2):
                            for i, r in enumerate(ROW_ORDER):
                                at, n, col = ROW_AT[r], (r + 1) * P, ROW_IN_BANK[r]
                                u = [k for k in range(3) if r in UNITS[k]][0]
                                if i == 0 and not begin:
                                    wait_alone(dve, p_exp, pair(8, b, p) - 4 + 4 * h)
                                wait_alone(dve, s_ps, pair(6, b, p) + 3 * h + u + 1)
                                dve.tensor_tensor_reduce(out=masked[:, h, at:at + n], in0=s_banks[u][:, col:col + n],
                                                         in1=mask_w[:, 512 - n:512], scale=-SCALE, scalar=BIG,
                                                         op0=ALU.add, op1=ALU.min,
                                                         accum_out=neg_max[:, 4 * h + r:4 * h + r + 1])\
                                    .then_inc(s_masked, 1)

                    def invert_sums(b, p):
                        for h in range(2):
                            dve.wait_ge(p_exp, pair(8, b, p) + 4 * h + 4)
                            dve.reciprocal(rdenom[:, 4 * h:4 * h + 4], denom[:, 4 * h:4 * h + 4]).then_inc(rden, 1)

                    def evac_z(b, p):
                        dve.wait_ge(z_ps, pair(1, b, p) + 1)
                        dve.tensor_copy(z_T[:, p, :], g_bank).then_inc(z_done, 1)

                    def add_attention(b):
                        dve.wait_ge(o_ps, b + 1)
                        dve.tensor_tensor(attn[:, :, :], g_bank.rearrange("p (t d) -> p t d", t=NT),
                                          bo_b[:, :].unsqueeze(1).broadcast_to([P, NT, D]), ALU.add).then_inc(o_biased, 1)
                        dve.wait_ge(o_biased, b + 1)
                        dve.tensor_tensor(attn[:, :, :], attn[:, :, :],
                                          gate_a[:, ds(b, 1), :].broadcast_to([P, NT, D]), ALU.mult).then_inc(o_gated, 1)
                        dve.wait_ge(o_gated, b + 1)
                        xs = x_all[:, ds(b * NT, NT), :]
                        dve.tensor_tensor(xs, xs, attn[:, :, :], ALU.add).then_inc(x_mid, 1)

                    ln_stats(0)
                    ln_apply(0)
                    split_h(0)
                    rest_qk(0, 0)

                    def body(b, first, last):
                        for p in range(NP):
                            begin = first and p == 0
                            if not (last and p == NP - 1):
                                rest_qk(*after(b, p))
                            if p == 6 and not last:
                                split_h(b + 1)
                            if not begin:
                                evac_T(*before(b, p), first and p == 1)
                            mask_and_max(b, p, begin)
                            if p == 1 and not first:
                                add_attention(b - 1)
                            invert_sums(b, p)
                            if not begin:
                                evac_z(*before(b, p))
                            if p == 3 and not last:
                                ln_stats(b + 1)
                            if p == 5 and not last:
                                ln_apply(b + 1)

                    batches(dve, body)
                    evac_T(B - 1, NP - 1, False)
                    evac_z(B - 1, NP - 1)
                    add_attention(B - 1)

        with ExitStack() as pb:
            def sbb(name, shape, dt=F32):
                return sb(name, shape, dt, pb)

            h_hi_all = sbb("h_hi_all", [P, B * S], F32R)
            h_lo_all = sbb("h_lo_all", [P, B * S], F32R)
            w1_hi = sbb("w1_hi", [P, E, H], F32R)
            w1_lo = sbb("w1_lo", [P, E, H], F32R)
            w2_sb = sbb("w2_sb", [P, E, HC, D])
            hidden = sbb("hidden", [P, 2, HC, S])
            w1_raw = hidden[:, :, :, :].rearrange("p a c s -> p (a c) s")
            wts = sbb("wts", [P, B * NT, E])
            logits = sbb("logits", [P, NT, E])
            top = sbb("top", [P, NT, E])
            chosen = sbb("chosen", [P, NT, E])
            shifted = sbb("shifted", [P, NT, E])
            expd = sbb("expd", [P, NT, E])
            kept = sbb("kept", [P, NT, E])
            w_now = sbb("w_now", [P, NT, E])
            w_sum = sbb("w_sum", [P, NT])
            w_rsum = sbb("w_rsum", [P, NT])
            w_T = sbb("w_T", [E, S])
            acc = sbb("acc", [P, NT, D])

            def tile_of(x, b, t):
                return x[:, ds(b * NT + t, 1), :].rearrange("p a d -> p (a d)")

            load_w1, load_w2, w1_split = sem("load_w1"), sem("load_w2"), sem("w1_split")
            r_stat, r_mv, r_eps, r_rstd, r_xn = (sem(f"r_{n}") for n in ("stat", "mv", "eps", "rstd", "xn"))
            r_T_ps, r_full, r_hi, r_lo = (sem(f"r_{n}") for n in ("T_ps", "full", "hi", "lo"))
            r_logit_ps, r_shift, r_exp, r_w, r_wT_ps, r_wT, r_b2_ps = (
                sem(f"r_{n}") for n in ("logit_ps", "shift", "exp", "w", "wT_ps", "wT", "b2_ps"))
            r_chain = sem("r_chain")

            with nc.Block() as block:
                @block.sync
                def _(sp):
                    sp.dma_start(w1_raw, W1.rearrange("e d h -> d e h")).then_inc(load_w1, 16)
                    sp.dma_start(w2_sb[:, :, :, :], W2.rearrange("e (c p) d -> p e c d", p=P)).then_inc(load_w2, 16)
                    sp.wait_ge(load_w2, 16)

                @block.vector
                def _(dve):
                    CHAIN = 7 + NT

                    with dve.Fori(0, B) as b:
                        links = [0]

                        def link(ins):
                            links[0] += 1
                            ins.then_inc(r_chain, 1)
                            wait_alone(dve, r_chain, CHAIN * b + links[0])

                        for t in range(NT):
                            dve.bn_stats(stats[:, t, :], tile_of(x_all, b, t)).then_inc(r_stat, 1)
                        for t in range(NT):
                            wait_alone(dve, r_stat, NT * b + t + 1)
                            dve.bn_aggr(meanvar[:, t, :], stats[:, t, :]).then_inc(r_mv, 1)
                        dve.wait_ge(r_rstd, b + 1)
                        for t in range(NT):
                            dve.tensor_scalar(xn[:, t, :], tile_of(x_all, b, t), meanvar[:, t, 0:1], rstd[:, t:t + 1],
                                              ALU.subtract, ALU.mult).then_inc(r_xn, 1)
                        dve.wait_ge(r_full, b + 1)
                        dve.tensor_copy(h_hi_all[:, ds(b * S, S)], hf[:, :]).then_inc(r_hi, 1)
                        dve.wait_ge(r_hi, b + 1)
                        dve.tensor_tensor(h_lo_all[:, ds(b * S, S)], hf[:, :], h_hi_all[:, ds(b * S, S)].bitcast(F32),
                                          ALU.subtract).then_inc(r_lo, 1)
                        dve.wait_ge(r_logit_ps, b + 1)
                        link(dve.tensor_tensor(logits[:, :, :], banks[:, 1, 0:NT * E].rearrange("p (t e) -> p t e", t=NT),
                                               br_b[:, :].unsqueeze(1).broadcast_to([P, NT, E]), ALU.add))
                        for t in range(NT):
                            link(dve.max(out=top[:, t, :], in_=logits[:, t, :]))
                        dve.tensor_tensor(shifted[:, :, :], logits[:, :, :],
                                          top[:, :, 0:1].broadcast_to([P, NT, E]), ALU.subtract).then_inc(r_shift, 1)
                        link(dve.tensor_tensor(chosen[:, :, :], logits[:, :, :],
                                               top[:, :, 1:2].broadcast_to([P, NT, E]), ALU.is_ge))
                        dve.wait_ge(r_exp, b + 1)
                        link(dve.tensor_tensor(kept[:, :, :], expd[:, :, :], chosen[:, :, :], ALU.mult))
                        link(dve.tensor_reduce(w_sum[:, :], kept[:, :, :], AX.X, ALU.add))
                        link(dve.reciprocal(w_rsum[:, :], w_sum[:, :]))
                        dve.tensor_tensor(w_now[:, :, :], kept[:, :, :],
                                          w_rsum[:, :].unsqueeze(2).broadcast_to([P, NT, E]), ALU.mult).then_inc(r_w, 1)
                        dve.tensor_tensor(wts[:, ds(b * NT, NT), :], kept[:, :, :],
                                          w_rsum[:, :].unsqueeze(2).broadcast_to([P, NT, E]), ALU.mult)
                        dve.wait_ge(r_wT_ps, b + 1)
                        dve.tensor_copy(w_T[:, :], banks[0:E, 2, :]).then_inc(r_wT, 1)
                        dve.wait_ge(r_b2_ps, b + 1)
                        link(dve.tensor_tensor(acc[:, :, :], banks[:, 3, :].rearrange("p (t d) -> p t d", t=NT),
                                               gate_b[:, ds(b, 1), :].broadcast_to([P, NT, D]), ALU.mult))
                        xs = x_all[:, ds(b * NT, NT), :]
                        dve.tensor_tensor(xs, xs, acc[:, :, :], ALU.add)
                        assert links[0] == CHAIN - 1
                        link(dve.memset(w_sum[:, :], 0.0))
                    dve.wait_ge(load_w1, 16)
                    dve.tensor_copy(w1_hi[:, :, :], w1_raw).then_inc(w1_split, 1)
                    dve.wait_ge(w1_split, 1)
                    dve.tensor_tensor(w1_lo[:, :, :], w1_raw, w1_hi[:, :, :].bitcast(F32), ALU.subtract)

                @block.gpsimd
                def _(pool):
                    with pool.Fori(0, B) as b:
                        wait_alone(pool, r_mv, NT * b + NT)
                        pool.tensor_scalar(var_eps[:, :], meanvar[:, :, 1], EPS, 1.0, ALU.add, ALU.mult).then_inc(r_eps, 1)
                        pool.wait_ge(r_eps, b + 1)
                        pool.tensor_tensor(rstd[:, :], var_eps[:, :], neg_half[:, :], ALU.pow).then_inc(r_rstd, 1)

                @block.scalar
                def _(act):
                    with act.Fori(0, B) as b:
                        act.wait_ge(r_T_ps, b + 1)
                        act.activation(hf[:, :], banks[:, 0, :], ACT.Identity, bias=mod_cols[:, 3, ds(b, 1)],
                                       scale=mod_cols[:, 4, ds(b, 1)]).then_inc(r_full, 1)
                        act.wait_ge(r_shift, b + 1)
                        act.activation(expd[:, :, :], shifted[:, :, :], ACT.Exp).then_inc(r_exp, 1)

                @block.tensor
                def _(pe):
                    with pe.Fori(0, B) as b:
                        pe.wait_ge(r_xn, NT * b + NT)
                        for t in range(NT):
                            mm = pe.transpose(banks[:, 0, t * P:(t + 1) * P], xn[:, t, :], ident[:, :])
                        mm.then_inc(r_T_ps, 1)
                        pe.wait_ge(r_full, b + 1)
                        for t in range(NT):
                            mm = pe.matmul(banks[:, 1, t * E:(t + 1) * E], hf[:, t * P:(t + 1) * P], wr_sb[:, :],
                                           start=True, stop=True)
                        mm.then_inc(r_logit_ps, 1)
                        pe.wait_ge(r_w, b + 1)
                        for t in range(NT):
                            mm = pe.matmul(banks[0:E, 2, t * P:(t + 1) * P], w_now[:, t, :], ident[:, :],
                                           start=True, stop=True)
                        mm.then_inc(r_wT_ps, 1)
                        pe.wait_ge(r_wT, b + 1)
                        for t in range(NT):
                            mm = pe.matmul(banks[:, 3, t * P:(t + 1) * P], w_T[:, t * P:(t + 1) * P], b2_rows[:, :],
                                           start=True, stop=True)
                        mm.then_inc(r_b2_ps, 1)

            hid_ps, hid, y_ps, y_acc = sem("hid_ps"), sem("hid"), sem("y_ps"), sem("y_acc")
            y_gated, y_out, stored = sem("y_gated"), sem("y_out"), sem("stored")
            y_result = sbb("y_result", [P, NT, D])

            with nc.Block() as block:
                @block.tensor
                def _(pe):
                    def first_layer(b, e, begin):
                        for c in range(HC):
                            if not begin:
                                pe.wait_ge(hid, HC * (E * b + e - 1) + c + 1)
                            cols = slice(c * P, (c + 1) * P)
                            h1, h2 = h_hi_all[:, ds(b * S, S)], h_lo_all[:, ds(b * S, S)]
                            pe.matmul(banks[:, c, :], w1_hi[:, e, cols], h1, start=True, stop=False)
                            pe.matmul(banks[:, c, :], w1_hi[:, e, cols], h2, start=False, stop=False)
                            pe.matmul(banks[:, c, :], w1_lo[:, e, cols], h1, start=False, stop=True).then_inc(hid_ps, 1)

                    def second_layer(b, e, begin):
                        pe.wait_ge(hid, HC * (E * b + e + 1))
                        if not begin:
                            pe.wait_ge(y_acc, NT * (E * b + e - 1))
                        for t in range(NT):
                            for c in range(HC):
                                mm = pe.matmul(banks[:, 4 + e % 2, t * P:(t + 1) * P], hidden[:, e % 2, c, t * P:(t + 1) * P],
                                               w2_sb[:, e, c, :], start=(c == 0), stop=(c == HC - 1))
                        mm.then_inc(y_ps, 1)

                    def body(b, first, last):
                        for e in range(E):
                            first_layer(b, e, first and e == 0)
                            if e > 0:
                                second_layer(b, e - 1, first and e < 3)
                        second_layer(b, E - 1, False)

                    batches(pe, body)

                @block.scalar
                def _(act):
                    def body(b, first, last):
                        for e in range(E):
                            if not (first and e < 2):
                                act.wait_ge(y_ps, E * b + e - 1)
                            for c in range(HC):
                                act.wait_ge(hid_ps, HC * (E * b + e) + c + 1)
                                act.activation(hidden[:, e % 2, c, :], banks[:, c, :], ACT.Gelu,
                                               bias=b1_cols[:, e * HC + c:e * HC + c + 1]).then_inc(hid, 1)

                    batches(act, body)

                @block.vector
                def _(dve):
                    def body(b, first, last):
                        if not first:
                            dve.wait_ge(y_out, b)
                        for e in range(E):
                            dve.wait_ge(y_ps, E * b + e + 1)
                            for t in range(NT):
                                y = banks[:, 4 + e % 2, t * P:(t + 1) * P]
                                w = wts[:, ds(b * NT + t, 1), e:e + 1].rearrange("p a e -> p (a e)")
                                if e == 0:
                                    dve.tensor_scalar(acc[:, t, :], y, w, None, ALU.mult).then_inc(y_acc, 1)
                                else:
                                    dve.wait_ge(y_acc, NT * (E * b + e - 1) + t + 1)
                                    dve.scalar_tensor_tensor(out=acc[:, t, :], in0=y, scalar=w, in1=acc[:, t, :],
                                                             op0=ALU.mult, op1=ALU.add).then_inc(y_acc, 1)
                        dve.wait_ge(y_acc, NT * E * b + NT * E)
                        dve.tensor_tensor(acc[:, :, :], acc[:, :, :],
                                          gate_b[:, ds(b, 1), :].broadcast_to([P, NT, D]), ALU.mult).then_inc(y_gated, 1)
                        dve.wait_ge(y_gated, b + 1)
                        if not first:
                            dve.wait_ge(stored, 16 * b)
                        dve.tensor_tensor(y_result[:, :, :], acc[:, :, :], x_all[:, ds(b * NT, NT), :], ALU.add)\
                            .then_inc(y_out, 1)

                    batches(dve, body)

                @block.sync
                def _(sp):
                    def body(b, first, last):
                        sp.wait_ge(y_out, b + 1)
                        sp.dma_start(out[ds(b, 1)].rearrange("b (t p) d -> p (b t) d", p=P), y_result[:, :, :])\
                            .then_inc(stored, 16)

                    batches(sp, body)
                    sp.wait_ge(stored, 16 * B)


_INS = ["L0_attn_resid", "L0_attn_W_Q", "L0_attn_W_K", "L0_attn_W_V", "L0_attn_W_out", "L0_attn_b_out",
        "L0_ffn_W1", "L0_ffn_b1", "L0_ffn_W2", "L0_ffn_b2", "L0_ffn_Wr", "L0_ffn_br", "L0_c", "L0_wmod"]


def kernel(**inputs):
    import numpy as _np
    import concourse.bacc as _bacc
    from concourse import mybir as _mybir
    from concourse.bass_utils import run_bass_kernel_spmd as _run

    nc = _bacc.Bacc("TRN2", target_bir_lowering=False, num_devices=1)
    arrays, args = {}, []
    for name in _INS:
        a = _np.ascontiguousarray(inputs[name])
        arrays[f"in_{name}_dram"] = a
        args.append(nc.dram_tensor(f"in_{name}_dram", a.shape, _mybir.dt.from_np(a.dtype), kind="ExternalInput").ap())
    shape = inputs["L0_attn_resid"].shape
    args.append(nc.dram_tensor("out_0_dram", shape, _mybir.dt.from_np(_np.dtype("float32")), kind="ExternalOutput").ap())
    adaln_moe_kernel(nc, *args)
    r = _run(nc, [arrays], core_ids=[0])
    return r.results[0]["out_0_dram"]
```

```python
from contextlib import ExitStack

import concourse.bass as bass
from concourse import mybir

F32 = mybir.dt.float32
F32R = mybir.dt.float32r
ALU = mybir.AluOpType
ACT = mybir.ActivationFunctionType
AX = mybir.AxisListType
ds = bass.ds

P = 128
EPS = 1e-5
NEG = -1e30
BIG = 3e38
GATE_MIN = 0.25

ROW_ORDER = [3, 2, 0, 1]
UNITS = [[3], [2, 0], [1]]
UNIT_END = [1, 3, 4]
ROW_AT = {3: 0, 2: 512, 0: 896, 1: 1024}
ROW_IN_BANK = {3: 0, 2: 0, 0: 384, 1: 0}
HEAD_COLS = 1280
V_CHUNKS = [[0, 1], [2, 3], [4], [5], [6], [7], [], []]
KEY_AT = {0: 0, 1: 512, 3: 896, 2: 1024}


def adaln_moe_kernel(nc, resid, W_Q, W_K, W_V, W_out, b_out, W1, b1, W2, b2, Wr, br, c_in, wmod, out):
    B, S, D = resid.shape
    NH, DH = W_Q.shape[1], W_Q.shape[2]
    E, _, H = W1.shape
    NT = S // P
    NP = NH // 2
    HC = H // P
    QK = NH * DH
    SCALE = float(DH) ** -0.5
    assert D == P and S == 512 and DH == 64 and NP == 8 and E == 8 and HC == 4 and B >= 3

    gates_dram = nc.dram_tensor("gates_dram", (B, 2 * D), F32, kind="Internal").ap()

    with ExitStack() as ctx:
        def sb(name, shape, dt=F32, at=ctx):
            return at.enter_context(nc.sbuf_tensor(name, shape, dt))

        def sem(name):
            return ctx.enter_context(nc.semaphore(name))

        banks = ctx.enter_context(nc.psum_tensor("banks", [P, 8, 512], F32))
        q_bank, k_bank = banks[:, 0, :], banks[:, 1, :]
        s_banks = [banks[:, 2 + i, :] for i in range(3)]
        t_banks = [banks[:, 5 + i, :] for i in range(2)]
        g_bank = banks[:, 7, :]

        x_all = sb("x_all", [P, B * NT, D])
        ident = sb("ident", [P, P])
        mod_cols = sb("mod_cols", [P, 6, B])
        gate_a = sb("gate_a", [P, B, D])
        gate_b = sb("gate_b", [P, B, D])
        neg_half = sb("neg_half", [P, NT])
        b1_cols = sb("b1_cols", [P, E * HC])
        b2_rows = sb("b2_rows", [E, D])
        wr_sb = sb("wr_sb", [D, E])
        br_b = sb("br_b", [P, E])
        stats = sb("stats", [P, NT, 6])
        meanvar = sb("meanvar", [P, NT, 2])
        var_eps = sb("var_eps", [P, NT])
        rstd = sb("rstd", [P, NT])
        xn = sb("xn", [P, NT, D])
        hf = sb("hf", [P, S])

        def pair(per, b, p):
            return per * NP * b + per * p

        def wait_alone(engine, semaphore, count):
            engine.wait_ge(semaphore, count)
            engine.nop(nofuse=True)

        def batches(engine, body):
            body(0, True, False)
            with engine.Fori(1, B - 1) as b:
                body(b, False, False)
            body(B - 1, False, True)

        def before(b, p):
            return (b, p - 1) if p > 0 else (b - 1, NP - 1)

        def two_before(b, p):
            return before(*before(b, p))

        def three_before(b, p):
            return before(*two_before(b, p))

        def after(b, p):
            return (b, p + 1) if p < NP - 1 else (b + 1, 0)

        x_in = sem("x_in")

        with ExitStack() as pa:
            def sa(name, shape, dt=F32):
                return sb(name, shape, dt, pa)

            wq = [sa("wq_hi", [P, QK], F32R), sa("wq_lo", [P, QK], F32R)]
            wk = [sa("wk_hi", [P, QK], F32R), sa("wk_lo", [P, QK], F32R)]
            wv = [sa("wv_hi", [P, QK], F32R), sa("wv_lo", [P, QK], F32R)]
            wo = sa("wo", [P, NP, D])
            bo_b = sa("bo_b", [P, D])
            q_split = sa("q_split", [P, 2, 2, S], F32R)
            k_hi2 = sa("k_hi2", [P, 2, 2, S], F32R)
            k_rest = sa("k_rest", [P, 2, 2, S], F32R)
            probs = sa("probs", [P, 2, 2, HEAD_COLS])
            probs_T = sa("probs_T", [P, 2, HEAD_COLS])
            v_sb = sa("v_sb", [P, NT, QK])
            z_T = sa("z_T", [P, NP, S])
            h_hi = sa("h_hi", [P, S], F32R)
            h_lo = sa("h_lo", [P, S], F32R)
            attn = sa("attn", [P, NT, D])
            mask_w = sa("mask_w", [P, 512])
            neg_max = sa("neg_max", [P, 2, 8])
            denom = sa("denom", [P, 2, 8])
            rdenom = sa("rdenom", [P, 2, 8])

            with ExitStack() as ps:
                raw_w = [v_sb[:, i, :] for i in range(3)]
                zv = z_T[:, :, :].rearrange("p a n -> p (a n)")
                wmod_sb = zv[:, 0:6 * D]
                c_rows = zv[0:B, 1024:1024 + D]
                b1_rows = zv[0:E * HC, 1152:1152 + P]
                c_cols = zv[:, 1280:1280 + B]
                e_c = zv[:, 1312:1312 + B]
                e1_c = zv[:, 1344:1344 + B]
                sig_c = zv[:, 1376:1376 + B]
                silu_c = zv[:, 1408:1408 + B]
                g_raw = zv[0:B, 1536:1536 + 2 * D]
                g_sign = zv[0:B, 2048:2048 + 2 * D]
                g_mag = zv[0:B, 2560:2560 + 2 * D]
                g_out = zv[0:B, 3072:3072 + 2 * D]

                load_rows = sem("load_rows")
                load_w = sem("load_w")
                load_mod = sem("load_mod")
                load_kept = sem("load_kept")
                pool_zero = sem("pool_zero")
                pool_const = sem("pool_const")
                cols_ps = sem("cols_ps")
                exp_c = sem("exp_c")
                dve_chain = sem("dve_chain")
                cols_ok = sem("cols_ok")
                silu_ok = sem("silu_ok")
                mod_ps = sem("mod_ps")
                gates_ok = sem("gates_ok")
                gates_out = sem("gates_out")
                gates_in = sem("gates_in")

                with nc.Block() as block:
                    @block.sync
                    def _(sp):
                        sp.dma_start(c_rows, c_in).then_inc(load_rows, 16)
                        sp.dma_start(b1_rows, b1.rearrange("e (c p) -> (e c) p", p=P)).then_inc(load_rows, 16)
                        sp.dma_start(wmod_sb, wmod).then_inc(load_mod, 16)
                        for dst, src in zip(raw_w, (W_Q, W_K, W_V)):
                            sp.dma_start(dst, src.rearrange("d h c -> d (h c)")).then_inc(load_w, 16)
                        sp.dma_start(x_all[:, 0:NT, :], resid[0].rearrange("(t p) d -> p t d", p=P)).then_inc(x_in, 16)
                        sp.wait_ge(gates_ok, 1)
                        sp.dma_start(gates_dram, g_out).then_inc(gates_out, 16)
                        sp.wait_ge(gates_out, 16)
                        gv = gates_dram.rearrange("b (g d) -> g b d", g=2)
                        for g, dst in enumerate((gate_a, gate_b)):
                            sp.dma_start(dst[:, :, :], gv[g].partition_broadcast(P)).then_inc(gates_in, 16)
                        sp.wait_ge(gates_in, 32)

                    @block.gpsimd
                    def _(pool):
                        pool.memset(ident[:, :], 0.0).then_inc(pool_zero, 1)
                        pool.memset(mask_w[:, :], 0.0).then_inc(pool_zero, 1)
                        pool.memset(neg_half[:, :], -0.5).then_inc(pool_const, 1)
                        pool.wait_ge(pool_zero, 2)
                        pool.affine_select(out=ident[:, :], in_=ident[:, :], compare_op=ALU.not_equal, fill=1.0,
                                           base=0, pattern=[[-1, P]], channel_multiplier=1).then_inc(pool_const, 1)
                        pool.affine_select(out=mask_w[:, 384:512], in_=mask_w[:, 384:512], compare_op=ALU.is_ge,
                                           fill=NEG, base=0, pattern=[[-1, P]], channel_multiplier=1)\
                            .then_inc(pool_const, 1)
                        pool.dma_start(bo_b[:, :], b_out.partition_broadcast(P)).then_inc(load_kept, 16)
                        pool.dma_start(br_b[:, :], br.partition_broadcast(P)).then_inc(load_kept, 16)
                        pool.dma_start(b2_rows[:, :], b2).then_inc(load_kept, 16)
                        pool.dma_start(wr_sb[:, :], Wr).then_inc(load_kept, 16)
                        wo_v = W_out.rearrange("c (n two) d -> two c n d", two=2)
                        for half in range(2):
                            pool.dma_start(wo[half * DH:(half + 1) * DH, :, :], wo_v[half]).then_inc(load_kept, 16)
                        pool.wait_ge(load_kept, 96)

                    @block.tensor
                    def _(pe):
                        pe.wait_ge(pool_const, 3)
                        pe.wait_ge(load_rows, 32)
                        pe.transpose(g_bank[:, 0:B], c_rows, ident[0:B, 0:B])
                        pe.transpose(g_bank[:, B:B + E * HC], b1_rows, ident[0:E * HC, 0:E * HC]).then_inc(cols_ps, 1)
                        pe.wait_ge(silu_ok, 1)
                        pe.wait_ge(load_mod, 16)
                        for j in range(6):
                            pe.matmul(s_banks[0][:, j * B:(j + 1) * B], wmod_sb[:, j * D:(j + 1) * D], silu_c,
                                      start=True, stop=True)
                        for g, j in enumerate((2, 5)):
                            mm = pe.matmul(s_banks[1][0:B, g * D:(g + 1) * D], silu_c, wmod_sb[:, j * D:(j + 1) * D],
                                           start=True, stop=True)
                        mm.then_inc(mod_ps, 1)

                    @block.scalar
                    def _(act):
                        act.wait_ge(cols_ok, 2)
                        act.activation(e_c, c_cols, ACT.Exp, scale=-1.0).then_inc(exp_c, 1)

                    @block.vector
                    def _(dve):
                        done = [0]

                        def link(ins):
                            done[0] += 1
                            ins.then_inc(dve_chain, 1)
                            dve.wait_ge(dve_chain, done[0])

                        dve.wait_ge(cols_ps, 1)
                        dve.tensor_copy(c_cols, g_bank[:, 0:B]).then_inc(cols_ok, 1)
                        dve.tensor_copy(b1_cols[:, :], g_bank[:, B:B + E * HC]).then_inc(cols_ok, 1)
                        dve.wait_ge(exp_c, 1)
                        link(dve.tensor_scalar(e1_c, e_c, 1.0, None, ALU.add))
                        link(dve.reciprocal(sig_c, e1_c))
                        dve.tensor_tensor(silu_c, c_cols, sig_c, ALU.mult).then_inc(silu_ok, 1)
                        dve.wait_ge(mod_ps, 1)
                        link(dve.tensor_copy(mod_cols[:, :, :].rearrange("p j b -> p (j b)"), s_banks[0][:, 0:6 * B]))
                        for j in (1, 4):
                            link(dve.tensor_scalar(mod_cols[:, j, :], mod_cols[:, j, :], 1.0, None, ALU.add))
                        link(dve.tensor_copy(g_raw, s_banks[1][0:B, 0:2 * D]))
                        link(dve.tensor_scalar(g_sign, g_raw, 0.0, 2.0, ALU.is_ge, ALU.mult))
                        link(dve.tensor_scalar(g_sign, g_sign, 1.0, None, ALU.subtract))
                        link(dve.tensor_tensor(g_mag, g_raw, g_sign, ALU.mult))
                        dve.scalar_tensor_tensor(out=g_out, in0=g_mag, scalar=GATE_MIN, in1=g_sign,
                                                 op0=ALU.max, op1=ALU.mult).then_inc(gates_ok, 1)
                        link(dve.memset(k_rest[:, :, :, :].rearrange("p a b n -> p (a b n)").bitcast(F32), 0.0))
                        dve.wait_ge(load_w, 48)
                        for (hi, lo), raw in zip((wq, wk, wv), raw_w):
                            link(dve.tensor_copy(hi[:, :], raw))
                            link(dve.tensor_tensor(lo[:, :], raw, hi[:, :].bitcast(F32), ALU.subtract))

            qk_ps = sem("qk_ps")
            s_ps = sem("s_ps")
            t_ps = sem("t_ps")
            z_ps = sem("z_ps")
            v_ps = sem("v_ps")
            lnT_ps = sem("lnT_ps")
            o_ps = sem("o_ps")
            q_hi = sem("q_hi")
            k_hi = sem("k_hi")
            t_act = sem("t_act")
            p_exp = sem("p_exp")
            v_done = sem("v_done")
            h_full = sem("h_full")
            q_lo = sem("q_lo")
            k_lo = sem("k_lo")
            t_dve = sem("t_dve")
            s_masked = sem("s_masked")
            rden = sem("rden")
            z_done = sem("z_done")
            ln_stat = sem("ln_stat")
            ln_mv = sem("ln_mv")
            ln_xn = sem("ln_xn")
            h_rounded = sem("h_rounded")
            h_rest = sem("h_rest")
            o_biased = sem("o_biased")
            o_gated = sem("o_gated")
            x_mid = sem("x_mid")
            p_norm = sem("p_norm")
            ln_eps = sem("ln_eps")
            ln_rstd = sem("ln_rstd")
            k_dup = [sem("k_dup0"), sem("k_dup1")]

            with nc.Block() as block:
                @block.sync
                def _(sp):
                    def dup(b, p):
                        for h in range(2):
                            src, dst = (0, DH) if h == 0 else (DH, 0)
                            sp.wait_ge(k_hi, pair(2, b, p) + h + 1)
                            sp.dma_start(k_hi2[dst:dst + DH, p % 2, h, :].bitcast(F32),
                                         k_hi2[src:src + DH, p % 2, h, :].bitcast(F32)).then_inc(k_dup[p % 2], 16)

                    def body(b, first, last):
                        if first:
                            dup(0, 0)
                        for p in range(NP):
                            if p == 0 and not last:
                                sp.wait_ge(x_in, 16 * b + 16)
                                sp.dma_start(x_all[:, ds((b + 1) * NT, NT), :],
                                             resid[ds(b + 1, 1)].rearrange("b (t p) d -> p (b t) d", p=P))\
                                    .then_inc(x_in, 16)
                            if not (last and p == NP - 1):
                                dup(*after(b, p))

                    batches(sp, body)

                @block.gpsimd
                def _(pool):
                    def inv_std(b):
                        wait_alone(pool, ln_mv, NT * b + NT)
                        pool.tensor_scalar(var_eps[:, :], meanvar[:, :, 1], EPS, 1.0, ALU.add, ALU.mult)\
                            .then_inc(ln_eps, 1)
                        pool.wait_ge(ln_eps, b + 1)
                        pool.tensor_tensor(rstd[:, :], var_eps[:, :], neg_half[:, :], ALU.pow).then_inc(ln_rstd, 1)

                    inv_std(0)

                    def body(b, first, last):
                        for p in range(NP):
                            if p == 5 and not last:
                                inv_std(b + 1)
                            for h in range(2):
                                wait_alone(pool, rden, pair(2, b, p) + h + 1)
                                for r in ROW_ORDER:
                                    at, n = ROW_AT[r], (r + 1) * P
                                    part = probs[:, p % 2, h, at:at + n]
                                    pool.tensor_scalar(part, part, rdenom[:, p % 2, 4 * h + r:4 * h + r + 1], 1.0,
                                                       ALU.mult, ALU.mult)\
                                        .then_inc(p_norm, 1)

                    batches(pool, body)

                @block.tensor
                def _(pe):
                    def split_product(ps, a, b):
                        pe.matmul(ps, a[0], b[0], start=True, stop=False)
                        pe.matmul(ps, a[1], b[0], start=False, stop=False)
                        return pe.matmul(ps, a[0], b[1], start=False, stop=True)

                    h_cols = (h_hi[:, :], h_lo[:, :])

                    def project(b, p, banks_free):
                        pe.wait_ge(h_rest, b + 1)
                        if banks_free is not None:
                            pe.wait_ge(*banks_free)
                        for w, bank, read in ((wq, q_bank, q_lo), (wk, k_bank, k_lo)):
                            if not isinstance(b, int) or b > 0 or p > 0:
                                pe.wait_ge(read, pair(2, b, p))
                            cols = slice(p * P, (p + 1) * P)
                            split_product(bank, (w[0][:, cols], w[1][:, cols]), h_cols).then_inc(qk_ps, 1)

                    def h_transposes(b):
                        pe.wait_ge(ln_xn, NT * b + NT)
                        for t in range(NT):
                            mm = pe.transpose(q_bank[:, t * P:(t + 1) * P], xn[:, t, :], ident[:, :])
                        mm.then_inc(lnT_ps, 1)

                    def scores(b, p, h, u, begin):
                        if h == 0 and u == 0:
                            pe.wait_ge(q_lo, pair(2, b, p) + 2)
                            pe.wait_ge(k_lo, pair(2, b, p) + 2)
                            pe.wait_ge(k_dup[p % 2], 128 * b + 32 * (p // 2) + 32)
                        if h == 1 or not begin:
                            pe.wait_ge(s_masked, pair(8, b, p) + 4 * (h - 1) + UNIT_END[u])
                        for r in UNITS[u]:
                            n = (r + 1) * P
                            at = ROW_IN_BANK[r]
                            ps = s_banks[u][:, at:at + n]
                            q = q_split[:, p % 2, h, r * P:(r + 1) * P]
                            pe.matmul(ps, q, k_hi2[:, p % 2, h, 0:n], start=True, stop=False)
                            mm = pe.matmul(ps, q, k_rest[:, p % 2, h, 0:n], start=False, stop=True)
                        mm.then_inc(s_ps, 1)

                    T_UNITS = [[(0, 0, r, r * P) for r in range(4)],
                               [(0, 1, r, (r - 1) * P) for r in range(1, 4)] + [(0, 3, 3, 384)],
                               [(1, 0, r, r * P) for r in range(4)],
                               [(1, 1, r, (r - 1) * P) for r in range(1, 4)] + [(1, 3, 3, 384)],
                               [(h, 2, r, 256 * h + (r - 2) * P) for h in range(2) for r in (2, 3)]]

                    def transposes(b, p, u, begin):
                        if u == 0:
                            pe.wait_ge(p_norm, pair(8, b, p) + 4)
                        if u == 2:
                            pe.wait_ge(p_norm, pair(8, b, p) + 8)
                        if u == 0 and not begin:
                            pe.wait_ge(t_act, pair(2, b, p))
                        if u == 1 and not begin:
                            pe.wait_ge(t_dve, pair(3, b, p))
                        if u == 2:
                            pe.wait_ge(t_dve, pair(3, b, p) + 1)
                        if u == 3:
                            pe.wait_ge(t_act, pair(2, b, p) + 1)
                        if u == 4:
                            pe.wait_ge(t_dve, pair(3, b, p) + 2)
                        bank = t_banks[(5 * p + u) % 2]
                        for h, c, r, at in T_UNITS[u]:
                            src = ROW_AT[r] + c * P
                            mm = pe.transpose(bank[:, at:at + P], probs[:, p % 2, h, src:src + P], ident[:, :])
                        mm.then_inc(t_ps, 1)

                    def weigh_values(b, p):
                        pe.wait_ge(t_dve, pair(3, b, p) + 3)
                        pe.wait_ge(t_act, pair(2, b, p) + 2)
                        pe.wait_ge(v_done, 8 * b + 4 + 4 * (p // 4))
                        if not isinstance(b, int) or b > 0 or p > 0:
                            pe.wait_ge(z_done, pair(1, b, p))
                        for c in range(NT):
                            for h in range(2):
                                n = S - c * P
                                hc = (2 * p + h) * DH
                                mm = pe.matmul(g_bank[h * DH:(h + 1) * DH, c * P:S], v_sb[:, c, hc:hc + DH],
                                               probs_T[:, h, KEY_AT[c]:KEY_AT[c] + n], start=(c == 0), stop=(c == NT - 1))
                        mm.then_inc(z_ps, 1)

                    def values(b, p, i):
                        t, half = i % 4, i // 4
                        pe.wait_ge((q_lo, k_lo)[i % 2], pair(2, b, p) + 4)
                        if i > 0:
                            pe.wait_ge(v_done, 8 * b + i - 1)
                        toks, cols = slice(t * P, (t + 1) * P), slice(half * 512, half * 512 + 512)
                        split_product((q_bank, k_bank)[i % 2], (h_hi[:, toks], h_lo[:, toks]),
                                      (wv[0][:, cols], wv[1][:, cols])).then_inc(v_ps, 1)

                    def project_out(b, t, k_taken):
                        if t == 0:
                            pe.wait_ge(z_done, pair(1, b, NP))
                            pe.wait_ge(k_lo, k_taken)
                        for p in range(NP):
                            mm = pe.matmul(k_bank[:, t * P:(t + 1) * P], z_T[:, p, t * P:(t + 1) * P], wo[:, p, :],
                                           start=(p == 0), stop=(p == NP - 1))
                        if t == NT - 1:
                            mm.then_inc(o_ps, 1)

                    def body(b, first, last):
                        if first:
                            h_transposes(0)
                            project(0, 0, None)
                        for p in range(NP):
                            begin = first and p == 0
                            prev, prev2 = before(b, p), two_before(b, p)
                            scores(b, p, 0, 0, begin)
                            if not (last and p == NP - 1):
                                if p > 0 and V_CHUNKS[p - 1]:
                                    banks_free = (v_done, 8 * b + V_CHUNKS[p - 1][-1] + 1)
                                else:
                                    banks_free = None
                                if p == 3 and not first:
                                    pe.wait_ge(o_biased, b)
                                project(*after(b, p), banks_free)
                            scores(b, p, 0, 1, begin)
                            scores(b, p, 0, 2, begin)
                            if not (first and p < 2):
                                weigh_values(*prev2)
                            out_tiles = list(range(NT)) if p == 2 and not first else []
                            if not begin:
                                transposes(*prev, 0, first and p == 1)
                                transposes(*prev, 1, first and p == 1)
                            scores(b, p, 1, 0, begin)
                            if not begin:
                                transposes(*prev, 2, False)
                            for i in V_CHUNKS[p]:
                                values(b, p, i)
                            if p == 6 and not last:
                                pe.wait_ge(q_lo, pair(2, b, p) + 4)
                                h_transposes(b + 1)
                            if out_tiles:
                                project_out(b - 1, out_tiles.pop(0), pair(2, b, p) + 4)
                            scores(b, p, 1, 1, begin)
                            if not begin:
                                transposes(*prev, 3, False)
                            if out_tiles:
                                project_out(b - 1, out_tiles.pop(0), pair(2, b, p) + 4)
                            scores(b, p, 1, 2, begin)
                            if not begin:
                                transposes(*prev, 4, False)
                            for t in out_tiles:
                                project_out(b - 1, t, None)

                    end = B - 1
                    batches(pe, body)
                    weigh_values(end, NP - 2)
                    for u in range(5):
                        transposes(end, NP - 1, u, False)
                    weigh_values(end, NP - 1)
                    for t in range(NT):
                        project_out(end, t, pair(2, end, NP))

                @block.scalar
                def _(act):
                    def h_evac(b):
                        act.wait_ge(lnT_ps, b + 1)
                        if not isinstance(b, int) or b > 0:
                            act.wait_ge(h_rest, b)
                        act.activation(hf[:, :], q_bank, ACT.Identity, bias=mod_cols[:, 0, ds(b, 1)],
                                       scale=mod_cols[:, 1, ds(b, 1)]).then_inc(h_full, 1)

                    def round_qk(b, p, reused):
                        for n, (dst, bank, done) in enumerate(((q_split, q_bank, q_hi), (k_hi2, k_bank, k_hi))):
                            act.wait_ge(qk_ps, pair(2, b, p) + n + 1)
                            if reused and n == 0:
                                act.wait_ge(s_ps, pair(6, b, p) - 6)
                            for h in range(2):
                                half = slice(h * DH, (h + 1) * DH)
                                act.activation(dst[half, p % 2, h, :], bank[half, :], ACT.Copy).then_inc(done, 1)

                    def evac_T(b, p, u, begin):
                        act.wait_ge(t_ps, pair(5, b, p) + u + 1)
                        if not begin:
                            act.wait_ge(z_ps, pair(1, b, p))
                        act.activation(probs_T[:, u // 2, 512:1024], t_banks[(5 * p + u) % 2], ACT.Copy)\
                            .then_inc(t_act, 1)

                    def exponentials(b, p, h, rows):
                        for r in rows:
                            i = 4 * h + ROW_ORDER.index(r)
                            at, n, col = ROW_AT[r], (r + 1) * P, 4 * h + r
                            act.wait_ge(s_masked, pair(8, b, p) + i + 1)
                            part = probs[:, p % 2, h, at:at + n]
                            act.activation(part, part, ACT.Exp, bias=neg_max[:, p % 2, col:col + 1], scale=-1.0,
                                           accum_out=denom[:, p % 2, col:col + 1]).then_inc(p_exp, 1)

                    h_evac(0)
                    round_qk(0, 0, False)

                    def body(b, first, last):
                        for p in range(NP):
                            begin = first and p == 0
                            prev = before(b, p)
                            if not (last and p == NP - 1):
                                round_qk(*after(b, p), not begin)
                            exponentials(b, p, 0, ROW_ORDER)
                            if not begin:
                                evac_T(*prev, 1, first and p == 1)
                            exponentials(b, p, 1, [3])
                            for i in V_CHUNKS[p]:
                                act.wait_ge(v_ps, 8 * b + i + 1)
                                act.activation(v_sb[:, i % 4, (i // 4) * 512:(i // 4) * 512 + 512],
                                               (q_bank, k_bank)[i % 2], ACT.Copy).then_inc(v_done, 1)
                            if p == 6 and not last:
                                h_evac(b + 1)
                            exponentials(b, p, 1, [2, 0])
                            if not begin:
                                evac_T(*prev, 3, False)
                            exponentials(b, p, 1, [1])

                    batches(act, body)
                    evac_T(B - 1, NP - 1, 1, False)
                    evac_T(B - 1, NP - 1, 3, False)

                @block.vector
                def _(dve):
                    def ln_stats(b):
                        dve.wait_ge(x_in, 16 * b + 16)
                        for t in range(NT):
                            dve.bn_stats(stats[:, t, :], x_all[:, ds(b * NT + t, 1), :].rearrange("p a d -> p (a d)"))\
                                .then_inc(ln_stat, 1)
                        for t in range(NT):
                            wait_alone(dve, ln_stat, NT * b + t + 1)
                            dve.bn_aggr(meanvar[:, t, :], stats[:, t, :]).then_inc(ln_mv, 1)

                    def ln_apply(b):
                        dve.wait_ge(ln_rstd, b + 1)
                        if not isinstance(b, int) or b > 0:
                            dve.wait_ge(lnT_ps, b)
                        for t in range(NT):
                            dve.tensor_scalar(xn[:, t, :], x_all[:, ds(b * NT + t, 1), :].rearrange("p a d -> p (a d)"),
                                              meanvar[:, t, 0:1], rstd[:, t:t + 1], ALU.subtract, ALU.mult)\
                                .then_inc(ln_xn, 1)

                    def split_h(b):
                        dve.wait_ge(h_full, b + 1)
                        if not isinstance(b, int) or b > 0:
                            dve.wait_ge(qk_ps, pair(2, b, 0))
                        dve.tensor_copy(h_hi[:, :], hf[:, :]).then_inc(h_rounded, 1)
                        dve.wait_ge(h_rounded, b + 1)
                        dve.tensor_tensor(h_lo[:, :], hf[:, :], h_hi[:, :].bitcast(F32), ALU.subtract).then_inc(h_rest, 1)

                    def rest_q(b, p, h):
                        own, other = slice(h * DH, (h + 1) * DH), slice((1 - h) * DH, (2 - h) * DH)
                        dve.wait_ge(q_hi, pair(2, b, p) + h + 1)
                        dve.tensor_tensor(q_split[other, p % 2, h, :], q_bank[own, :],
                                          q_split[own, p % 2, h, :].bitcast(F32), ALU.subtract).then_inc(q_lo, 1)

                    def rest_k(b, p, h):
                        own = slice(h * DH, (h + 1) * DH)
                        dve.wait_ge(k_hi, pair(2, b, p) + h + 1)
                        dve.tensor_tensor(k_rest[own, p % 2, h, :], k_bank[own, :],
                                          k_hi2[own, p % 2, h, :].bitcast(F32), ALU.subtract).then_inc(k_lo, 1)

                    def evac_T(b, p, u, begin):
                        dve.wait_ge(t_ps, pair(5, b, p) + u + 1)
                        if not begin:
                            dve.wait_ge(z_ps, pair(1, b, p))
                        bank = t_banks[(5 * p + u) % 2]
                        if u < 4:
                            dst, src = probs_T[:, u // 2, 0:512], bank
                        else:
                            dst, src = probs_T[:, :, 1024:1280], bank.rearrange("p (h n) -> p h n", h=2)
                        dve.tensor_copy(dst, src).then_inc(t_dve, 1)

                    def mask_and_max(b, p, h, u, early):
                        if h == 0 and u == 0 and not early:
                            wait_alone(dve, t_ps, pair(5, b, p) - 5)
                        wait_alone(dve, s_ps, pair(6, b, p) + 3 * h + u + 1)
                        for r in UNITS[u]:
                            at, n, col = ROW_AT[r], (r + 1) * P, ROW_IN_BANK[r]
                            dve.tensor_tensor_reduce(out=probs[:, p % 2, h, at:at + n], in0=s_banks[u][:, col:col + n],
                                                     in1=mask_w[:, 512 - n:512], scale=-SCALE, scalar=BIG,
                                                     op0=ALU.add, op1=ALU.min,
                                                     accum_out=neg_max[:, p % 2, 4 * h + r:4 * h + r + 1])\
                                .then_inc(s_masked, 1)

                    def invert_sums(b, p, h):
                        dve.wait_ge(p_exp, pair(8, b, p) + 4 * h + 4)
                        dve.reciprocal(rdenom[:, p % 2, 4 * h:4 * h + 4], denom[:, p % 2, 4 * h:4 * h + 4])\
                            .then_inc(rden, 1)

                    def evac_z(b, p):
                        dve.wait_ge(z_ps, pair(1, b, p) + 1)
                        dve.tensor_copy(z_T[:, p, :], g_bank).then_inc(z_done, 1)

                    def add_bias(b):
                        dve.wait_ge(o_ps, b + 1)
                        dve.tensor_tensor(attn[:, :, :], k_bank.rearrange("p (t d) -> p t d", t=NT),
                                          bo_b[:, :].unsqueeze(1).broadcast_to([P, NT, D]), ALU.add).then_inc(o_biased, 1)

                    def add_attention(b):
                        dve.wait_ge(o_biased, b + 1)
                        dve.tensor_tensor(attn[:, :, :], attn[:, :, :],
                                          gate_a[:, ds(b, 1), :].broadcast_to([P, NT, D]), ALU.mult).then_inc(o_gated, 1)
                        dve.wait_ge(o_gated, b + 1)
                        xs = x_all[:, ds(b * NT, NT), :]
                        dve.tensor_tensor(xs, xs, attn[:, :, :], ALU.add).then_inc(x_mid, 1)

                    ln_stats(0)
                    ln_apply(0)
                    split_h(0)
                    for h in range(2):
                        rest_q(0, 0, h)
                    for h in range(2):
                        rest_k(0, 0, h)

                    def body(b, first, last):
                        for p in range(NP):
                            begin = first and p == 0
                            early = first and p < 2
                            prev = before(b, p)
                            has_next = not (last and p == NP - 1)
                            if p == 3 and not first:
                                add_bias(b - 1)
                            if not (first and p < 3):
                                evac_z(*three_before(b, p))
                            if not begin:
                                invert_sums(*prev, 1)
                            mask_and_max(b, p, 0, 0, early)
                            if has_next:
                                rest_q(*after(b, p), 0)
                            mask_and_max(b, p, 0, 1, early)
                            if has_next:
                                rest_q(*after(b, p), 1)
                            mask_and_max(b, p, 0, 2, early)
                            if has_next:
                                rest_k(*after(b, p), 0)
                            if not begin:
                                evac_T(*prev, 0, first and p == 1)
                            if has_next:
                                rest_k(*after(b, p), 1)
                            mask_and_max(b, p, 1, 0, early)
                            invert_sums(b, p, 0)
                            if not begin:
                                evac_T(*prev, 2, False)
                            if p == 6 and not last:
                                split_h(b + 1)
                            mask_and_max(b, p, 1, 1, early)
                            mask_and_max(b, p, 1, 2, early)
                            if not begin:
                                evac_T(*prev, 4, False)
                            if p == 3 and not first:
                                add_attention(b - 1)
                            if p == 4 and not last:
                                ln_stats(b + 1)
                            if p == 5 and not last:
                                ln_apply(b + 1)

                    batches(dve, body)
                    end = B - 1
                    evac_z(end, NP - 3)
                    invert_sums(end, NP - 1, 1)
                    evac_z(end, NP - 2)
                    for u in (0, 2, 4):
                        evac_T(end, NP - 1, u, False)
                    evac_z(end, NP - 1)
                    add_bias(end)
                    add_attention(end)

        with ExitStack() as pb:
            def sbb(name, shape, dt=F32):
                return sb(name, shape, dt, pb)

            h_hi_all = sbb("h_hi_all", [P, B * S], F32R)
            h_lo_all = sbb("h_lo_all", [P, B * S], F32R)
            w1_hi = sbb("w1_hi", [P, E, H], F32R)
            w1_lo = sbb("w1_lo", [P, E, H], F32R)
            w2_sb = sbb("w2_sb", [P, E, HC, D])
            hidden = sbb("hidden", [P, 2, HC, S])
            w1_raw = hidden[:, :, :, :].rearrange("p a c s -> p (a c) s")
            assert H == S and E == 2 * HC
            wts = sbb("wts", [P, B * NT, E])
            logits = sbb("logits", [P, NT, E])
            top = sbb("top", [P, NT, E])
            chosen = sbb("chosen", [P, NT, E])
            shifted = sbb("shifted", [P, NT, E])
            expd = sbb("expd", [P, NT, E])
            kept = sbb("kept", [P, NT, E])
            w_now = sbb("w_now", [P, NT, E])
            w_sum = sbb("w_sum", [P, NT])
            w_rsum = sbb("w_rsum", [P, NT])
            w_T = sbb("w_T", [E, S])
            b2_part = sbb("b2_part", [P, NT, D])
            acc = sbb("acc", [P, NT, D])
            y_result = sbb("y_result", [P, NT, D])
            hT_bank, wT_bank = banks[:, 6, :], banks[0:E, 6, :]
            logit_bank, b2_bank = banks[:, 7, 0:NT * E], banks[:, 7, :]

            def tile_of(x, b, t):
                return x[:, ds(b * NT + t, 1), :].rearrange("p a d -> p (a d)")

            load_w1 = [sem(f"load_w1_{i}") for i in range(E)]
            load_w2, w1_hi_ok, w1_split = sem("load_w2"), sem("w1_hi_ok"), sem("w1_split")
            r_stat, r_mv, r_eps, r_rstd, r_xn = (sem(f"r_{n}") for n in ("stat", "mv", "eps", "rstd", "xn"))
            r_T_ps, r_full, r_hi, r_lo = (sem(f"r_{n}") for n in ("T_ps", "full", "hi", "lo"))
            r_logit_ps, r_shift, r_exp, r_w, r_wT_ps, r_wT, r_b2_ps, r_wts, r_x = (
                sem(f"r_{n}") for n in ("logit_ps", "shift", "exp", "w", "wT_ps", "wT", "b2_ps", "wts", "x"))
            r_chain = sem("r_chain")
            hid_ps, hid, y_ps, y_acc = sem("hid_ps"), sem("hid"), sem("y_ps"), sem("y_acc")
            y_gated, y_out, stored = sem("y_gated"), sem("y_out"), sem("stored")

            with nc.Block() as block:
                @block.tensor
                def _(pe):
                    def route(b, stage):
                        if stage == 0:
                            pe.wait_ge(r_xn, NT * b + NT)
                            for t in range(NT):
                                mm = pe.transpose(hT_bank[:, t * P:(t + 1) * P], xn[:, t, :], ident[:, :])
                            mm.then_inc(r_T_ps, 1)
                        if stage == 1:
                            pe.wait_ge(r_full, b + 1)
                            for t in range(NT):
                                mm = pe.matmul(logit_bank[:, t * E:(t + 1) * E], hf[:, t * P:(t + 1) * P],
                                               wr_sb[:, :], start=True, stop=True)
                            mm.then_inc(r_logit_ps, 1)
                        if stage == 2:
                            pe.wait_ge(r_w, b + 1)
                            for t in range(NT):
                                mm = pe.matmul(wT_bank[:, t * P:(t + 1) * P], w_now[:, t, :], ident[:, :],
                                               start=True, stop=True)
                            mm.then_inc(r_wT_ps, 1)
                        if stage == 3:
                            pe.wait_ge(r_wT, b + 1)
                            for t in range(NT):
                                mm = pe.matmul(b2_bank[:, t * P:(t + 1) * P], w_T[:, t * P:(t + 1) * P],
                                               b2_rows[:, :], start=True, stop=True)
                            mm.then_inc(r_b2_ps, 1)

                    def first_layer(b, e, begin):
                        if e == 0:
                            pe.wait_ge(r_lo, b + 1)
                        for c in range(HC):
                            if not begin:
                                pe.wait_ge(hid, HC * (E * b + e - 1) + c + 1)
                            cols = slice(c * P, (c + 1) * P)
                            h1, h2 = h_hi_all[:, ds(b * S, S)], h_lo_all[:, ds(b * S, S)]
                            pe.matmul(banks[:, c, :], w1_hi[:, e, cols], h1, start=True, stop=False)
                            pe.matmul(banks[:, c, :], w1_hi[:, e, cols], h2, start=False, stop=False)
                            pe.matmul(banks[:, c, :], w1_lo[:, e, cols], h1, start=False, stop=True).then_inc(hid_ps, 1)

                    def second_layer(b, e, begin):
                        pe.wait_ge(hid, HC * (E * b + e + 1))
                        if not begin:
                            pe.wait_ge(y_acc, NT * (E * b + e - 1))
                        for t in range(NT):
                            for c in range(HC):
                                mm = pe.matmul(banks[:, 4 + e % 2, t * P:(t + 1) * P], hidden[:, e % 2, c, t * P:(t + 1) * P],
                                               w2_sb[:, e, c, :], start=(c == 0), stop=(c == HC - 1))
                        mm.then_inc(y_ps, 1)

                    def body(b, first, last):
                        for e in range(E):
                            if first:
                                pe.wait_ge(w1_split, e + 1)
                            first_layer(b, e, first and e == 0)
                            if first and e == 1:
                                pe.wait_ge(load_w2, 16)
                            if e > 0:
                                second_layer(b, e - 1, first and e < 3)
                            if e == 1:
                                route(b, 3)
                            if not last and e in (3, 4):
                                route(b + 1, e - 3)
                        second_layer(b, E - 1, False)
                        if not last:
                            route(b + 1, 2)

                    for stage in range(3):
                        route(0, stage)
                    batches(pe, body)

                @block.gpsimd
                def _(pool):
                    def inv_std(b):
                        wait_alone(pool, r_mv, NT * b + NT)
                        pool.tensor_scalar(var_eps[:, :], meanvar[:, :, 1], EPS, 1.0, ALU.add, ALU.mult).then_inc(r_eps, 1)
                        pool.wait_ge(r_eps, b + 1)
                        pool.tensor_tensor(rstd[:, :], var_eps[:, :], neg_half[:, :], ALU.pow).then_inc(r_rstd, 1)

                    inv_std(0)
                    with pool.Fori(1, B) as b:
                        inv_std(b)

                @block.scalar
                def _(act):
                    def h_evac(b):
                        act.wait_ge(r_T_ps, b + 1)
                        act.activation(hf[:, :], hT_bank, ACT.Identity, bias=mod_cols[:, 3, ds(b, 1)],
                                       scale=mod_cols[:, 4, ds(b, 1)]).then_inc(r_full, 1)

                    def logit_exp(b):
                        act.wait_ge(r_shift, b + 1)
                        act.activation(expd[:, :, :], shifted[:, :, :], ACT.Exp).then_inc(r_exp, 1)

                    def body(b, first, last):
                        for e in range(E):
                            if not (first and e < 2):
                                act.wait_ge(y_ps, E * b + e - 1)
                            if first and e < 2:
                                act.wait_ge(w1_split, HC * (e + 1))
                            for c in range(HC):
                                act.wait_ge(hid_ps, HC * (E * b + e) + c + 1)
                                act.activation(hidden[:, e % 2, c, :], banks[:, c, :], ACT.Gelu,
                                               bias=b1_cols[:, e * HC + c:e * HC + c + 1]).then_inc(hid, 1)
                            if e == 3 and not last:
                                h_evac(b + 1)
                            if e == 6 and not last:
                                logit_exp(b + 1)

                    h_evac(0)
                    logit_exp(0)
                    batches(act, body)

                @block.vector
                def _(dve):
                    CHAIN = 6 + NT
                    links = [0]

                    def link(b, ins):
                        links[0] += 1
                        ins.then_inc(r_chain, 1)
                        wait_alone(dve, r_chain, CHAIN * b + links[0])

                    def norm_stats(b):
                        links[0] = 0
                        for t in range(NT):
                            dve.bn_stats(stats[:, t, :], tile_of(x_all, b, t)).then_inc(r_stat, 1)
                        for t in range(NT):
                            wait_alone(dve, r_stat, NT * b + t + 1)
                            dve.bn_aggr(meanvar[:, t, :], stats[:, t, :]).then_inc(r_mv, 1)

                    def norm_rows(b):
                        dve.wait_ge(r_rstd, b + 1)
                        for t in range(NT):
                            dve.tensor_scalar(xn[:, t, :], tile_of(x_all, b, t), meanvar[:, t, 0:1], rstd[:, t:t + 1],
                                              ALU.subtract, ALU.mult).then_inc(r_xn, 1)

                    def split_h(b):
                        dve.wait_ge(r_full, b + 1)
                        dve.tensor_copy(h_hi_all[:, ds(b * S, S)], hf[:, :]).then_inc(r_hi, 1)
                        dve.wait_ge(r_hi, b + 1)
                        dve.tensor_tensor(h_lo_all[:, ds(b * S, S)], hf[:, :], h_hi_all[:, ds(b * S, S)].bitcast(F32),
                                          ALU.subtract).then_inc(r_lo, 1)

                    def choose(b):
                        dve.wait_ge(r_logit_ps, b + 1)
                        link(b, dve.tensor_tensor(logits[:, :, :], logit_bank.rearrange("p (t e) -> p t e", t=NT),
                                                  br_b[:, :].unsqueeze(1).broadcast_to([P, NT, E]), ALU.add))
                        for t in range(NT):
                            link(b, dve.max(out=top[:, t, :], in_=logits[:, t, :]))
                        dve.tensor_tensor(shifted[:, :, :], logits[:, :, :],
                                          top[:, :, 0:1].broadcast_to([P, NT, E]), ALU.subtract).then_inc(r_shift, 1)
                        link(b, dve.tensor_tensor(chosen[:, :, :], logits[:, :, :],
                                                  top[:, :, 1:2].broadcast_to([P, NT, E]), ALU.is_ge))

                    def weights(b):
                        dve.wait_ge(r_exp, b + 1)
                        link(b, dve.tensor_tensor(kept[:, :, :], expd[:, :, :], chosen[:, :, :], ALU.mult))
                        link(b, dve.tensor_reduce(w_sum[:, :], kept[:, :, :], AX.X, ALU.add))
                        link(b, dve.reciprocal(w_rsum[:, :], w_sum[:, :]))
                        rsum = w_rsum[:, :].unsqueeze(2).broadcast_to([P, NT, E])
                        dve.tensor_tensor(w_now[:, :, :], kept[:, :, :], rsum, ALU.mult).then_inc(r_w, 1)
                        dve.tensor_tensor(wts[:, ds(b * NT, NT), :], kept[:, :, :], rsum, ALU.mult).then_inc(r_wts, 1)

                    def weights_T(b):
                        dve.wait_ge(r_wT_ps, b + 1)
                        dve.tensor_copy(w_T[:, :], wT_bank).then_inc(r_wT, 1)

                    def add_b2(b):
                        dve.wait_ge(r_b2_ps, b + 1)
                        link(b, dve.tensor_tensor(b2_part[:, :, :], b2_bank.rearrange("p (t d) -> p t d", t=NT),
                                                  gate_b[:, ds(b, 1), :].broadcast_to([P, NT, D]), ALU.mult))
                        xs = x_all[:, ds(b * NT, NT), :]
                        dve.tensor_tensor(xs, xs, b2_part[:, :, :], ALU.add).then_inc(r_x, 1)
                        wait_alone(dve, r_x, b + 1)
                        assert links[0] == CHAIN

                    def split_w1(e):
                        dve.wait_ge(load_w1[e], 16)
                        dve.tensor_copy(w1_hi[:, e, :], w1_raw[:, e, :]).then_inc(w1_hi_ok, 1)
                        dve.wait_ge(w1_hi_ok, e + 1)
                        dve.tensor_tensor(w1_lo[:, e, :], w1_raw[:, e, :], w1_hi[:, e, :].bitcast(F32),
                                          ALU.subtract).then_inc(w1_split, 1)

                    STEPS = [norm_stats, norm_rows, None, split_h, choose, None, weights, weights_T]

                    def body(b, first, last):
                        if not first:
                            dve.wait_ge(y_out, b)
                        dve.wait_ge(r_wts, b + 1)
                        for e in range(E):
                            dve.wait_ge(y_ps, E * b + e + 1)
                            for t in range(NT):
                                y = banks[:, 4 + e % 2, t * P:(t + 1) * P]
                                w = wts[:, ds(b * NT + t, 1), e:e + 1].rearrange("p a e -> p (a e)")
                                if e == 0:
                                    dve.tensor_scalar(acc[:, t, :], y, w, None, ALU.mult).then_inc(y_acc, 1)
                                else:
                                    dve.wait_ge(y_acc, NT * (E * b + e - 1) + t + 1)
                                    dve.scalar_tensor_tensor(out=acc[:, t, :], in0=y, scalar=w, in1=acc[:, t, :],
                                                             op0=ALU.mult, op1=ALU.add).then_inc(y_acc, 1)
                            if e == 0:
                                add_b2(b)
                            if not last and STEPS[e]:
                                STEPS[e](b + 1)
                        dve.wait_ge(y_acc, NT * E * b + NT * E)
                        dve.tensor_tensor(acc[:, :, :], acc[:, :, :],
                                          gate_b[:, ds(b, 1), :].broadcast_to([P, NT, D]), ALU.mult).then_inc(y_gated, 1)
                        dve.wait_ge(y_gated, b + 1)
                        dve.wait_ge(r_x, b + 1)
                        if not first:
                            dve.wait_ge(stored, 16 * b)
                        dve.tensor_tensor(y_result[:, :, :], acc[:, :, :], x_all[:, ds(b * NT, NT), :], ALU.add)\
                            .then_inc(y_out, 1)

                    norm_stats(0)
                    norm_rows(0)
                    split_h(0)
                    choose(0)
                    weights(0)
                    weights_T(0)
                    for e in range(E):
                        split_w1(e)
                    batches(dve, body)

                @block.sync
                def _(sp):
                    for e in range(E):
                        sp.dma_start(w1_raw[:, e, :], W1[e]).then_inc(load_w1[e], 16)
                    sp.dma_start(w2_sb[:, :, :, :], W2.rearrange("e (c p) d -> p e c d", p=P)).then_inc(load_w2, 16)

                    def body(b, first, last):
                        sp.wait_ge(y_out, b + 1)
                        sp.dma_start(out[ds(b, 1)].rearrange("b (t p) d -> p (b t) d", p=P), y_result[:, :, :])\
                            .then_inc(stored, 16)

                    batches(sp, body)
                    sp.wait_ge(stored, 16 * B)


_INS = ["L0_attn_resid", "L0_attn_W_Q", "L0_attn_W_K", "L0_attn_W_V", "L0_attn_W_out", "L0_attn_b_out",
        "L0_ffn_W1", "L0_ffn_b1", "L0_ffn_W2", "L0_ffn_b2", "L0_ffn_Wr", "L0_ffn_br", "L0_c", "L0_wmod"]


def kernel(**inputs):
    import numpy as _np
    import concourse.bacc as _bacc
    from concourse import mybir as _mybir
    from concourse.bass_utils import run_bass_kernel_spmd as _run

    nc = _bacc.Bacc("TRN2", target_bir_lowering=False, num_devices=1)
    arrays, args = {}, []
    for name in _INS:
        a = _np.ascontiguousarray(inputs[name])
        arrays[f"in_{name}_dram"] = a
        args.append(nc.dram_tensor(f"in_{name}_dram", a.shape, _mybir.dt.from_np(a.dtype), kind="ExternalInput").ap())
    shape = inputs["L0_attn_resid"].shape
    args.append(nc.dram_tensor("out_0_dram", shape, _mybir.dt.from_np(_np.dtype("float32")), kind="ExternalOutput").ap())
    adaln_moe_kernel(nc, *args)
    r = _run(nc, [arrays], core_ids=[0])
    return r.results[0]["out_0_dram"]
```

```python
from contextlib import ExitStack

import concourse.bass as bass
from concourse import mybir

F32 = mybir.dt.float32
F32R = mybir.dt.float32r
ALU = mybir.AluOpType
ACT = mybir.ActivationFunctionType
AX = mybir.AxisListType
ds = bass.ds

P = 128
EPS = 1e-5
NEG = -1e30
BIG = 3e38
GATE_MIN = 0.25

ROW_ORDER = [3, 2, 0, 1]
UNITS = [[3], [2, 0], [1]]
UNIT_END = [1, 3, 4]
ROW_AT = {3: 0, 2: 512, 0: 896, 1: 1024}
ROW_IN_BANK = {3: 0, 2: 0, 0: 384, 1: 0}
HEAD_COLS = 1280
V_CHUNKS = [[0, 1], [2, 3], [4], [5, 6], [7], [], [], []]
KEY_AT = {0: 0, 1: 512, 3: 896, 2: 1024}


def adaln_moe_kernel(nc, resid, W_Q, W_K, W_V, W_out, b_out, W1, b1, W2, b2, Wr, br, c_in, wmod, out):
    B, S, D = resid.shape
    NH, DH = W_Q.shape[1], W_Q.shape[2]
    E, _, H = W1.shape
    NT = S // P
    NP = NH // 2
    HC = H // P
    QK = NH * DH
    SCALE = float(DH) ** -0.5
    assert D == P and S == 512 and DH == 64 and NP == 8 and E == 8 and HC == 4 and B >= 3

    with ExitStack() as ctx:
        def sb(name, shape, dt=F32, at=ctx):
            return at.enter_context(nc.sbuf_tensor(name, shape, dt))

        def sem(name):
            return ctx.enter_context(nc.semaphore(name))

        banks = ctx.enter_context(nc.psum_tensor("banks", [P, 8, 512], F32))
        q_bank, k_bank = banks[:, 0, :], banks[:, 1, :]
        s_banks = [banks[:, 2 + i, :] for i in range(3)]
        t_banks = [banks[:, 5 + i, :] for i in range(2)]
        g_bank = banks[:, 7, :]

        x_all = sb("x_all", [P, B * NT, D])
        ident = sb("ident", [P, P])
        mod_cols = sb("mod_cols", [P, 6, B])
        gate_cols = sb("gate_cols", [P, 2, B])
        neg_half = sb("neg_half", [P, NT])
        b1_cols = sb("b1_cols", [P, E * HC])
        b2_rows = sb("b2_rows", [E, D])
        wr_sb = sb("wr_sb", [D, E])
        br_b = sb("br_b", [P, E])
        stats = sb("stats", [P, NT, 6])
        meanvar = sb("meanvar", [P, NT, 2])
        var_eps = sb("var_eps", [P, NT])
        rstd = sb("rstd", [P, NT])
        xn = sb("xn", [P, NT, D])
        hf = sb("hf", [P, S])

        def pair(per, b, p):
            return per * NP * b + per * p

        def wait_alone(engine, semaphore, count):
            engine.wait_ge(semaphore, count)
            engine.nop(nofuse=True)

        def batches(engine, body):
            body(0, True, False)
            with engine.Fori(1, B - 1) as b:
                body(b, False, False)
            body(B - 1, False, True)

        def before(b, p):
            return (b, p - 1) if p > 0 else (b - 1, NP - 1)

        def two_before(b, p):
            return before(*before(b, p))

        def three_before(b, p):
            return before(*two_before(b, p))

        def after(b, p):
            return (b, p + 1) if p < NP - 1 else (b + 1, 0)

        x_in = sem("x_in")

        with ExitStack() as pa:
            def sa(name, shape, dt=F32):
                return sb(name, shape, dt, pa)

            wq = [sa("wq_hi", [P, QK], F32R), sa("wq_lo", [P, QK], F32R)]
            wk = [sa("wk_hi", [P, QK], F32R), sa("wk_lo", [P, QK], F32R)]
            wv = [sa("wv_hi", [P, QK], F32R), sa("wv_lo", [P, QK], F32R)]
            wo = [sa("wo_hi", [P, NP, D], F32R), sa("wo_lo", [P, NP, D], F32R)]
            bo_col = sa("bo_col", [P, 1])
            q_split = sa("q_split", [P, 2, 2, S], F32R)
            k_hi2 = sa("k_hi2", [P, 2, 2, S], F32R)
            k_own = sa("k_own", [P, 2, S], F32R)
            k_rest = sa("k_rest", [P, 2, S], F32R)
            probs = sa("probs", [P, 2, 2, HEAD_COLS])
            probs_T = sa("probs_T", [P, 2, HEAD_COLS])
            v_sb = sa("v_sb", [P, NT, QK])
            z_hi = sa("z_hi", [P, NP, S], F32R)
            z_lo = sa("z_lo", [P, NP, S], F32R)
            h_hi = sa("h_hi", [P, S], F32R)
            h_lo = sa("h_lo", [P, S], F32R)
            attn_T = sa("attn_T", [P, S])
            mask_w = sa("mask_w", [P, 512])
            neg_max = sa("neg_max", [P, 2, 8])
            denom = sa("denom", [P, 2, 8])
            rdenom = sa("rdenom", [P, 2, 8])

            with ExitStack() as ps:
                raw_w = [v_sb[:, i, :] for i in range(3)]
                raw_wo = v_sb[:, 3, :]
                zv = probs[:, :, :, :].rearrange("p a b n -> p (a b n)")
                wmod_sb = zv[:, 0:6 * D]
                c_rows = zv[0:B, 1024:1024 + D]
                b1_rows = zv[0:E * HC, 1152:1152 + P]
                c_cols = zv[:, 1280:1280 + B]
                e_c = zv[:, 1312:1312 + B]
                e1_c = zv[:, 1344:1344 + B]
                sig_c = zv[:, 1376:1376 + B]
                silu_c = zv[:, 1408:1408 + B]
                g_sign = [zv[:, 1440:1440 + B], zv[:, 1472:1472 + B]]
                g_mag = [zv[:, 1504:1504 + B], zv[:, 1536:1536 + B]]

                flat_w = [tuple(w[:, :] for w in pair_w) for pair_w in (wq, wk, wv)]
                flat_w.append(tuple(w[:, :, :].rearrange("p n d -> p (n d)") for w in wo))

                load_rows = sem("load_rows")
                load_w = [sem(f"load_w_{n}") for n in "qkvo"]
                w_rounded = sem("w_rounded")
                load_mod = sem("load_mod")
                load_kept = sem("load_kept")
                pool_zero = sem("pool_zero")
                pool_const = sem("pool_const")
                cols_ps = sem("cols_ps")
                exp_c = sem("exp_c")
                dve_chain = sem("dve_chain")
                cols_ok = sem("cols_ok")
                silu_ok = sem("silu_ok")
                mod_ps = sem("mod_ps")
                gates_ok = sem("gates_ok")

                with nc.Block() as block:
                    @block.sync
                    def _(sp):
                        sp.dma_start(x_all[:, 0:NT, :], resid[0].rearrange("(t p) d -> p t d", p=P)).then_inc(x_in, 16)
                        sp.dma_start(c_rows, c_in).then_inc(load_rows, 16)
                        sp.dma_start(b1_rows, b1.rearrange("e (c p) -> (e c) p", p=P)).then_inc(load_rows, 16)
                        sp.dma_start(wmod_sb, wmod).then_inc(load_mod, 16)
                        for dst, src, load in zip(raw_w, (W_Q, W_K, W_V), load_w):
                            sp.dma_start(dst, src.rearrange("d h c -> d (h c)")).then_inc(load, 16)
                    @block.gpsimd
                    def _(pool):
                        pool.memset(ident[:, :], 0.0).then_inc(pool_zero, 1)
                        pool.memset(mask_w[:, :], 0.0).then_inc(pool_zero, 1)
                        pool.memset(neg_half[:, :], -0.5).then_inc(pool_const, 1)
                        pool.wait_ge(pool_zero, 2)
                        pool.affine_select(out=ident[:, :], in_=ident[:, :], compare_op=ALU.not_equal, fill=1.0,
                                           base=0, pattern=[[-1, P]], channel_multiplier=1).then_inc(pool_const, 1)
                        pool.affine_select(out=mask_w[:, 384:512], in_=mask_w[:, 384:512], compare_op=ALU.is_ge,
                                           fill=NEG, base=0, pattern=[[-1, P]], channel_multiplier=1)\
                            .then_inc(pool_const, 1)
                        pool.dma_start(bo_col[:, :], b_out.rearrange("(d o) -> d o", o=1)).then_inc(load_kept, 16)
                        pool.dma_start(br_b[:, :], br.partition_broadcast(P)).then_inc(load_kept, 16)
                        pool.dma_start(b2_rows[:, :], b2).then_inc(load_kept, 16)
                        pool.dma_start(wr_sb[:, :], Wr).then_inc(load_kept, 16)
                        wo_v = W_out.rearrange("c (n two) d -> two c n d", two=2)
                        for half in range(2):
                            pool.dma_start(raw_wo[half * DH:(half + 1) * DH, :].rearrange("p (n d) -> p n d", n=NP),
                                           wo_v[half]).then_inc(load_w[3], 16)
                        pool.wait_ge(load_kept, 64)

                    @block.tensor
                    def _(pe):
                        pe.wait_ge(pool_const, 3)
                        pe.wait_ge(load_rows, 32)
                        pe.transpose(g_bank[:, 0:B], c_rows, ident[0:B, 0:B])
                        pe.transpose(g_bank[:, B:B + E * HC], b1_rows, ident[0:E * HC, 0:E * HC]).then_inc(cols_ps, 1)
                        pe.wait_ge(silu_ok, 1)
                        pe.wait_ge(load_mod, 16)
                        for j in range(6):
                            mm = pe.matmul(s_banks[0][:, j * B:(j + 1) * B], wmod_sb[:, j * D:(j + 1) * D], silu_c,
                                           start=True, stop=True)
                        mm.then_inc(mod_ps, 1)

                    @block.scalar
                    def _(act):
                        act.wait_ge(cols_ok, 2)
                        act.activation(e_c, c_cols, ACT.Exp, scale=-1.0).then_inc(exp_c, 1)
                        for (hi, lo), raw, load, n in zip(flat_w, raw_w + [raw_wo], load_w, (1, 1, 1, 2)):
                            act.wait_ge(load, 16 * n)
                            act.activation(hi, raw, ACT.Copy).then_inc(w_rounded, 1)

                    @block.vector
                    def _(dve):
                        done = [0]

                        def link(ins):
                            done[0] += 1
                            ins.then_inc(dve_chain, 1)
                            dve.wait_ge(dve_chain, done[0])

                        dve.wait_ge(cols_ps, 1)
                        dve.tensor_copy(c_cols, g_bank[:, 0:B]).then_inc(cols_ok, 1)
                        dve.tensor_copy(b1_cols[:, :], g_bank[:, B:B + E * HC]).then_inc(cols_ok, 1)
                        dve.wait_ge(exp_c, 1)
                        link(dve.tensor_scalar(e1_c, e_c, 1.0, None, ALU.add))
                        link(dve.reciprocal(sig_c, e1_c))
                        dve.tensor_tensor(silu_c, c_cols, sig_c, ALU.mult).then_inc(silu_ok, 1)
                        dve.wait_ge(mod_ps, 1)
                        link(dve.tensor_copy(mod_cols[:, :, :].rearrange("p j b -> p (j b)"), s_banks[0][:, 0:6 * B]))
                        for j in (1, 4):
                            link(dve.tensor_scalar(mod_cols[:, j, :], mod_cols[:, j, :], 1.0, None, ALU.add))
                        for g, j in enumerate((2, 5)):
                            raw, sign, mag = mod_cols[:, j, :], g_sign[g], g_mag[g]
                            link(dve.tensor_scalar(sign, raw, 0.0, 2.0, ALU.is_ge, ALU.mult))
                            link(dve.tensor_scalar(sign, sign, 1.0, None, ALU.subtract))
                            link(dve.tensor_tensor(mag, raw, sign, ALU.mult))
                            dve.scalar_tensor_tensor(out=gate_cols[:, g, :], in0=mag, scalar=GATE_MIN, in1=sign,
                                                     op0=ALU.max, op1=ALU.mult).then_inc(gates_ok, 1)
                        for i, ((hi, lo), raw) in enumerate(zip(flat_w, raw_w + [raw_wo])):
                            dve.wait_ge(w_rounded, i + 1)
                            link(dve.tensor_tensor(lo, raw, hi.bitcast(F32), ALU.subtract))

            qk_ps = sem("qk_ps")
            s_ps = sem("s_ps")
            t_ps = sem("t_ps")
            z_ps = sem("z_ps")
            v_ps = sem("v_ps")
            lnT_ps = sem("lnT_ps")
            o_ps = sem("o_ps")
            oT_ps = sem("oT_ps")
            q_hi = sem("q_hi")
            k_hi = sem("k_hi")
            t_act = sem("t_act")
            p_exp = sem("p_exp")
            v_done = sem("v_done")
            h_full = sem("h_full")
            h_rounded = sem("h_rounded")
            z_rounded = sem("z_rounded")
            q_lo = sem("q_lo")
            k_lo = sem("k_lo")
            t_dve = sem("t_dve")
            s_masked = sem("s_masked")
            rden = sem("rden")
            z_done = sem("z_done")
            ln_stat = sem("ln_stat")
            ln_mv = sem("ln_mv")
            ln_xn = sem("ln_xn")
            h_rest = sem("h_rest")
            o_gated = sem("o_gated")
            x_mid = sem("x_mid")
            p_norm = sem("p_norm")
            ln_eps = sem("ln_eps")
            ln_rstd = sem("ln_rstd")
            k_dup = [sem("k_dup0"), sem("k_dup1")]

            with nc.Block() as block:
                @block.sync
                def _(sp):
                    def dup(b, p):
                        sp.wait_ge(k_hi, pair(1, b, p) + 1)
                        for h in range(2):
                            own = slice(h * DH, (h + 1) * DH)
                            for dst in (slice(0, DH), slice(DH, P)):
                                sp.dma_start(k_hi2[dst, p % 2, h, :].bitcast(F32), k_own[own, p % 2, :].bitcast(F32))\
                                    .then_inc(k_dup[p % 2], 16)

                    def body(b, first, last):
                        if first:
                            dup(0, 0)
                        for p in range(NP):
                            if p == 0 and not last:
                                sp.wait_ge(x_in, 16 * b + 16)
                                sp.dma_start(x_all[:, ds((b + 1) * NT, NT), :],
                                             resid[ds(b + 1, 1)].rearrange("b (t p) d -> p (b t) d", p=P))\
                                    .then_inc(x_in, 16)
                            if not (last and p == NP - 1):
                                dup(*after(b, p))

                    batches(sp, body)

                @block.gpsimd
                def _(pool):
                    def inv_std(b):
                        wait_alone(pool, ln_mv, NT * b + NT)
                        pool.tensor_scalar(var_eps[:, :], meanvar[:, :, 1], EPS, 1.0, ALU.add, ALU.mult)\
                            .then_inc(ln_eps, 1)
                        pool.wait_ge(ln_eps, b + 1)
                        pool.tensor_tensor(rstd[:, :], var_eps[:, :], neg_half[:, :], ALU.pow).then_inc(ln_rstd, 1)

                    inv_std(0)

                    def body(b, first, last):
                        for p in range(NP):
                            if p == 3 and not last:
                                inv_std(b + 1)
                            for h in range(2):
                                wait_alone(pool, rden, pair(2, b, p) + h + 1)
                                for r in ROW_ORDER:
                                    at, n = ROW_AT[r], (r + 1) * P
                                    part = probs[:, p % 2, h, at:at + n]
                                    pool.tensor_scalar(part, part, rdenom[:, p % 2, 4 * h + r:4 * h + r + 1], 1.0,
                                                       ALU.mult, ALU.mult)\
                                        .then_inc(p_norm, 1)

                    batches(pool, body)

                @block.tensor
                def _(pe):
                    def split_product(ps, a, b):
                        pe.matmul(ps, a[0], b[0], start=True, stop=False)
                        pe.matmul(ps, a[1], b[0], start=False, stop=False)
                        return pe.matmul(ps, a[0], b[1], start=False, stop=True)

                    h_cols = (h_hi[:, :], h_lo[:, :])

                    def project(b, p, banks_free, k_free=None):
                        pe.wait_ge(h_rest, b + 1)
                        if banks_free is not None:
                            pe.wait_ge(*banks_free)
                        for w, bank, read, per in ((wq, q_bank, q_lo, 2), (wk, k_bank, k_lo, 1)):
                            if not isinstance(b, int) or b > 0 or p > 0:
                                pe.wait_ge(read, pair(per, b, p))
                            if w is wk and k_free is not None:
                                pe.wait_ge(*k_free)
                            cols = slice(p * P, (p + 1) * P)
                            split_product(bank, (w[0][:, cols], w[1][:, cols]), h_cols).then_inc(qk_ps, 1)

                    def h_transposes(b):
                        pe.wait_ge(ln_xn, NT * b + NT)
                        for t in range(NT):
                            mm = pe.transpose(q_bank[:, t * P:(t + 1) * P], xn[:, t, :], ident[:, :])
                        mm.then_inc(lnT_ps, 1)

                    def scores(b, p, h, u, begin):
                        if h == 0 and u == 0:
                            pe.wait_ge(q_lo, pair(2, b, p) + 2)
                            pe.wait_ge(k_lo, pair(1, b, p) + 1)
                            pe.wait_ge(k_dup[p % 2], 256 * b + 64 * (p // 2) + 64)
                        if h == 1 or not begin:
                            pe.wait_ge(s_masked, pair(8, b, p) + 4 * (h - 1) + UNIT_END[u])
                        for r in UNITS[u]:
                            n = (r + 1) * P
                            at = ROW_IN_BANK[r]
                            ps = s_banks[u][:, at:at + n]
                            rows, own = slice(r * P, (r + 1) * P), slice(h * DH, (h + 1) * DH)
                            pe.matmul(ps, q_split[:, p % 2, h, rows], k_hi2[:, p % 2, h, 0:n], start=True, stop=False)
                            mm = pe.matmul(ps, q_split[own, p % 2, h, rows], k_rest[own, p % 2, 0:n],
                                           start=False, stop=True)
                        mm.then_inc(s_ps, 1)

                    T_UNITS = [[(0, 0, r, r * P) for r in range(4)],
                               [(0, 1, r, (r - 1) * P) for r in range(1, 4)] + [(0, 3, 3, 384)],
                               [(1, 0, r, r * P) for r in range(4)],
                               [(1, 1, r, (r - 1) * P) for r in range(1, 4)] + [(1, 3, 3, 384)],
                               [(h, 2, r, 256 * h + (r - 2) * P) for h in range(2) for r in (2, 3)]]

                    def transposes(b, p, u, begin):
                        if u == 0:
                            pe.wait_ge(p_norm, pair(8, b, p) + 4)
                        if u == 2:
                            pe.wait_ge(p_norm, pair(8, b, p) + 8)
                        if u == 0 and not begin:
                            pe.wait_ge(t_act, pair(2, b, p))
                        if u == 1 and not begin:
                            pe.wait_ge(t_dve, pair(3, b, p))
                        if u == 2:
                            pe.wait_ge(t_dve, pair(3, b, p) + 1)
                        if u == 3:
                            pe.wait_ge(t_act, pair(2, b, p) + 1)
                        if u == 4:
                            pe.wait_ge(t_dve, pair(3, b, p) + 2)
                        bank = t_banks[(5 * p + u) % 2]
                        for h, c, r, at in T_UNITS[u]:
                            src = ROW_AT[r] + c * P
                            mm = pe.transpose(bank[:, at:at + P], probs[:, p % 2, h, src:src + P], ident[:, :])
                        mm.then_inc(t_ps, 1)

                    def weigh_values(b, p):
                        pe.wait_ge(t_dve, pair(3, b, p) + 3)
                        pe.wait_ge(t_act, pair(2, b, p) + 2)
                        pe.wait_ge(v_done, 8 * b + 4 + 4 * (p // 4))
                        if not isinstance(b, int) or b > 0 or p > 0:
                            pe.wait_ge(z_done, pair(1, b, p))
                        for c in range(NT):
                            for h in range(2):
                                n = S - c * P
                                hc = (2 * p + h) * DH
                                mm = pe.matmul(g_bank[h * DH:(h + 1) * DH, c * P:S], v_sb[:, c, hc:hc + DH],
                                               probs_T[:, h, KEY_AT[c]:KEY_AT[c] + n], start=(c == 0), stop=(c == NT - 1))
                        mm.then_inc(z_ps, 1)

                    def values(b, p, n, i):
                        t, half = i % 4, i // 4
                        if n == 0:
                            pe.wait_ge(q_lo, pair(2, b, p) + 4)
                        else:
                            pe.wait_ge(k_lo, pair(1, b, p) + 2)
                        if i > 0:
                            pe.wait_ge(v_done, 8 * b + i - 1)
                        toks, cols = slice(t * P, (t + 1) * P), slice(half * 512, half * 512 + 512)
                        split_product((q_bank, k_bank)[n], (h_hi[:, toks], h_lo[:, toks]),
                                      (wv[0][:, cols], wv[1][:, cols])).then_inc(v_ps, 1)

                    def project_out(b, part, k_taken):
                        if part == 0:
                            pe.wait_ge(z_done, pair(1, b, NP))
                            pe.wait_ge(k_lo, k_taken)
                        for p in range(2 * part, 2 * part + 2):
                            pe.matmul(k_bank, wo[0][:, p, :], z_hi[:, p, :], start=(p == 0), stop=False)
                            pe.matmul(k_bank, wo[1][:, p, :], z_hi[:, p, :], start=False, stop=False)
                            mm = pe.matmul(k_bank, wo[0][:, p, :], z_lo[:, p, :], start=False, stop=(p == NP - 1))
                        if part == NT - 1:
                            mm.then_inc(o_ps, 1)

                    def attention_T(b, k_taken):
                        pe.wait_ge(o_gated, b + 1)
                        if k_taken is not None:
                            pe.wait_ge(k_lo, k_taken)
                        for t in range(NT):
                            mm = pe.transpose(k_bank[:, t * P:(t + 1) * P], attn_T[:, t * P:(t + 1) * P], ident[:, :])
                        mm.then_inc(oT_ps, 1)

                    def body(b, first, last):
                        if first:
                            h_transposes(0)
                            project(0, 0, None)
                        for p in range(NP):
                            begin = first and p == 0
                            prev, prev2 = before(b, p), two_before(b, p)
                            scores(b, p, 0, 0, begin)
                            if not (last and p == NP - 1):
                                if p > 0 and V_CHUNKS[p - 1]:
                                    banks_free = (v_done, 8 * b + V_CHUNKS[p - 1][-1] + 1)
                                elif p == 6 and not last:
                                    banks_free = (h_full, b + 2)
                                else:
                                    banks_free = None
                                k_free = {3: (o_gated, b), 5: (x_mid, b)}.get(p) if not first else None
                                project(*after(b, p), banks_free, k_free)
                            scores(b, p, 0, 1, begin)
                            scores(b, p, 0, 2, begin)
                            if not (first and p < 2):
                                weigh_values(*prev2)
                            out_parts = list(range(NT)) if p == 2 and not first else []
                            if not begin:
                                transposes(*prev, 0, first and p == 1)
                                transposes(*prev, 1, first and p == 1)
                            scores(b, p, 1, 0, begin)
                            for n, i in enumerate(V_CHUNKS[p]):
                                values(b, p, n, i)
                            if not begin:
                                transposes(*prev, 2, False)
                            if p == 5 and not last:
                                pe.wait_ge(q_lo, pair(2, b, p) + 4)
                                h_transposes(b + 1)
                            if out_parts:
                                project_out(b - 1, out_parts.pop(0), pair(1, b, p) + 2)
                            scores(b, p, 1, 1, begin)
                            if not begin:
                                transposes(*prev, 3, False)
                            if p == 4 and not first:
                                attention_T(b - 1, pair(1, b, p) + 2)
                            if out_parts:
                                project_out(b - 1, out_parts.pop(0), pair(1, b, p) + 2)
                            scores(b, p, 1, 2, begin)
                            if not begin:
                                transposes(*prev, 4, False)
                            for part in out_parts:
                                project_out(b - 1, part, None)

                    end = B - 1
                    batches(pe, body)
                    weigh_values(end, NP - 2)
                    for u in range(5):
                        transposes(end, NP - 1, u, False)
                    weigh_values(end, NP - 1)
                    for part in range(NT):
                        project_out(end, part, pair(1, end, NP))
                    attention_T(end, None)

                @block.scalar
                def _(act):
                    def h_evac(b):
                        act.wait_ge(lnT_ps, b + 1)
                        if not isinstance(b, int) or b > 0:
                            act.wait_ge(h_rest, b)
                        act.activation(hf[:, :], q_bank, ACT.Identity, bias=mod_cols[:, 0, ds(b, 1)],
                                       scale=mod_cols[:, 1, ds(b, 1)]).then_inc(h_full, 1)

                    def round_qk(b, p, reused):
                        act.wait_ge(qk_ps, pair(2, b, p) + 1)
                        if reused:
                            act.wait_ge(s_ps, pair(6, b, p) - 6)
                        for h in range(2):
                            half = slice(h * DH, (h + 1) * DH)
                            act.activation(q_split[half, p % 2, h, :], q_bank[half, :], ACT.Copy).then_inc(q_hi, 1)
                        act.wait_ge(qk_ps, pair(2, b, p) + 2)
                        act.activation(k_own[:, p % 2, :], k_bank, ACT.Copy).then_inc(k_hi, 1)

                    def evac_T(b, p, u, begin):
                        act.wait_ge(t_ps, pair(5, b, p) + u + 1)
                        if not begin:
                            act.wait_ge(z_ps, pair(1, b, p))
                        act.activation(probs_T[:, u // 2, 512:1024], t_banks[(5 * p + u) % 2], ACT.Copy)\
                            .then_inc(t_act, 1)

                    def exponentials(b, p, h, rows):
                        for r in rows:
                            i = 4 * h + ROW_ORDER.index(r)
                            at, n, col = ROW_AT[r], (r + 1) * P, 4 * h + r
                            act.wait_ge(s_masked, pair(8, b, p) + i + 1)
                            part = probs[:, p % 2, h, at:at + n]
                            act.activation(part, part, ACT.Exp, bias=neg_max[:, p % 2, col:col + 1], scale=-1.0,
                                           accum_out=denom[:, p % 2, col:col + 1]).then_inc(p_exp, 1)

                    def round_h(b):
                        act.wait_ge(h_full, b + 1)
                        if not isinstance(b, int) or b > 0:
                            act.wait_ge(qk_ps, pair(2, b, 0))
                        act.activation(h_hi[:, :], hf[:, :], ACT.Copy).then_inc(h_rounded, 1)

                    def round_z(b, p):
                        act.wait_ge(z_ps, pair(1, b, p) + 1)
                        if p == 0 and (not isinstance(b, int) or b > 0):
                            act.wait_ge(o_ps, b)
                        act.activation(z_hi[:, p, :], g_bank, ACT.Copy).then_inc(z_rounded, 1)

                    h_evac(0)
                    round_h(0)
                    round_qk(0, 0, False)

                    def body(b, first, last):
                        for p in range(NP):
                            begin = first and p == 0
                            prev = before(b, p)
                            if not (last and p == NP - 1):
                                round_qk(*after(b, p), not begin)
                            exponentials(b, p, 0, ROW_ORDER)
                            if not begin:
                                evac_T(*prev, 1, first and p == 1)
                            if not (first and p < 2) and p != 2:
                                round_z(*two_before(b, p))
                            exponentials(b, p, 1, [3])
                            for n, i in enumerate(V_CHUNKS[p]):
                                act.wait_ge(v_ps, 8 * b + i + 1)
                                act.activation(v_sb[:, i % 4, (i // 4) * 512:(i // 4) * 512 + 512],
                                               (q_bank, k_bank)[n], ACT.Copy).then_inc(v_done, 1)
                            if p == 5 and not last:
                                h_evac(b + 1)
                            if p == 6 and not last:
                                round_h(b + 1)
                            exponentials(b, p, 1, [2, 0])
                            if not begin:
                                evac_T(*prev, 3, False)
                            exponentials(b, p, 1, [1])
                            if p == 2:
                                round_z(*two_before(b, p))

                    batches(act, body)
                    round_z(B - 1, NP - 2)
                    evac_T(B - 1, NP - 1, 1, False)
                    evac_T(B - 1, NP - 1, 3, False)
                    round_z(B - 1, NP - 1)

                @block.vector
                def _(dve):
                    def ln_stats(b):
                        dve.wait_ge(x_in, 16 * b + 16)
                        for t in range(NT):
                            dve.bn_stats(stats[:, t, :], x_all[:, ds(b * NT + t, 1), :].rearrange("p a d -> p (a d)"))\
                                .then_inc(ln_stat, 1)
                        for t in range(NT):
                            wait_alone(dve, ln_stat, NT * b + t + 1)
                            dve.bn_aggr(meanvar[:, t, :], stats[:, t, :]).then_inc(ln_mv, 1)

                    def ln_apply(b):
                        dve.wait_ge(ln_rstd, b + 1)
                        if not isinstance(b, int) or b > 0:
                            dve.wait_ge(lnT_ps, b)
                        for t in range(NT):
                            dve.tensor_scalar(xn[:, t, :], x_all[:, ds(b * NT + t, 1), :].rearrange("p a d -> p (a d)"),
                                              meanvar[:, t, 0:1], rstd[:, t:t + 1], ALU.subtract, ALU.mult)\
                                .then_inc(ln_xn, 1)

                    def rest_h(b):
                        dve.wait_ge(h_rounded, b + 1)
                        dve.tensor_tensor(h_lo[:, :], hf[:, :], h_hi[:, :].bitcast(F32), ALU.subtract).then_inc(h_rest, 1)

                    def rest_q(b, p, h):
                        own, other = slice(h * DH, (h + 1) * DH), slice((1 - h) * DH, (2 - h) * DH)
                        dve.wait_ge(q_hi, pair(2, b, p) + h + 1)
                        dve.tensor_tensor(q_split[other, p % 2, h, :], q_bank[own, :],
                                          q_split[own, p % 2, h, :].bitcast(F32), ALU.subtract).then_inc(q_lo, 1)

                    def rest_k(b, p):
                        dve.wait_ge(k_hi, pair(1, b, p) + 1)
                        dve.tensor_tensor(k_rest[:, p % 2, :], k_bank, k_own[:, p % 2, :].bitcast(F32),
                                          ALU.subtract).then_inc(k_lo, 1)

                    def evac_T(b, p, u, begin):
                        dve.wait_ge(t_ps, pair(5, b, p) + u + 1)
                        if not begin:
                            dve.wait_ge(z_ps, pair(1, b, p))
                        bank = t_banks[(5 * p + u) % 2]
                        if u < 4:
                            dst, src = probs_T[:, u // 2, 0:512], bank
                        else:
                            dst, src = probs_T[:, :, 1024:1280], bank.rearrange("p (h n) -> p h n", h=2)
                        dve.tensor_copy(dst, src).then_inc(t_dve, 1)

                    def mask_and_max(b, p, h, u, early):
                        if h == 0 and u == 0 and not early:
                            wait_alone(dve, t_ps, pair(5, b, p) - 5)
                        wait_alone(dve, s_ps, pair(6, b, p) + 3 * h + u + 1)
                        for r in UNITS[u]:
                            at, n, col = ROW_AT[r], (r + 1) * P, ROW_IN_BANK[r]
                            dve.tensor_tensor_reduce(out=probs[:, p % 2, h, at:at + n], in0=s_banks[u][:, col:col + n],
                                                     in1=mask_w[:, 512 - n:512], scale=-SCALE, scalar=BIG,
                                                     op0=ALU.add, op1=ALU.min,
                                                     accum_out=neg_max[:, p % 2, 4 * h + r:4 * h + r + 1])\
                                .then_inc(s_masked, 1)

                    def invert_sums(b, p, h):
                        dve.wait_ge(p_exp, pair(8, b, p) + 4 * h + 4)
                        dve.reciprocal(rdenom[:, p % 2, 4 * h:4 * h + 4], denom[:, p % 2, 4 * h:4 * h + 4])\
                            .then_inc(rden, 1)

                    def rest_z(b, p):
                        dve.wait_ge(z_rounded, pair(1, b, p) + 1)
                        dve.tensor_tensor(z_lo[:, p, :], g_bank, z_hi[:, p, :].bitcast(F32), ALU.subtract)\
                            .then_inc(z_done, 1)

                    def gate_attention(b):
                        dve.wait_ge(o_ps, b + 1)
                        if not isinstance(b, int) or b > 0:
                            dve.wait_ge(oT_ps, b)
                        dve.tensor_scalar(attn_T[:, :], k_bank, bo_col[:, :], gate_cols[:, 0, ds(b, 1)],
                                          ALU.add, ALU.mult).then_inc(o_gated, 1)

                    def add_attention(b):
                        dve.wait_ge(oT_ps, b + 1)
                        xs = x_all[:, ds(b * NT, NT), :]
                        dve.tensor_tensor(xs, k_bank.rearrange("p (t d) -> p t d", t=NT), xs, ALU.add)\
                            .then_inc(x_mid, 1)

                    ln_stats(0)
                    ln_apply(0)
                    rest_h(0)
                    for h in range(2):
                        rest_q(0, 0, h)
                    rest_k(0, 0)

                    def body(b, first, last):
                        for p in range(NP):
                            begin = first and p == 0
                            early = first and p < 2
                            prev = before(b, p)
                            has_next = not (last and p == NP - 1)
                            if p == 3 and not first:
                                gate_attention(b - 1)
                            if not (first and p < 3):
                                rest_z(*three_before(b, p))
                            if not begin:
                                invert_sums(*prev, 1)
                            mask_and_max(b, p, 0, 0, early)
                            if has_next:
                                rest_q(*after(b, p), 0)
                            mask_and_max(b, p, 0, 1, early)
                            if has_next:
                                rest_q(*after(b, p), 1)
                            mask_and_max(b, p, 0, 2, early)
                            if not begin:
                                evac_T(*prev, 0, first and p == 1)
                            if has_next:
                                rest_k(*after(b, p))
                            mask_and_max(b, p, 1, 0, early)
                            invert_sums(b, p, 0)
                            if not begin:
                                evac_T(*prev, 2, False)
                            mask_and_max(b, p, 1, 1, early)
                            mask_and_max(b, p, 1, 2, early)
                            if p == 6 and not last:
                                rest_h(b + 1)
                            if not begin:
                                evac_T(*prev, 4, False)
                            if p == 4 and not first:
                                add_attention(b - 1)
                            if p == 2 and not last:
                                ln_stats(b + 1)
                            if p == 3 and not last:
                                ln_apply(b + 1)

                    batches(dve, body)
                    end = B - 1
                    rest_z(end, NP - 3)
                    invert_sums(end, NP - 1, 1)
                    rest_z(end, NP - 2)
                    for u in (0, 2, 4):
                        evac_T(end, NP - 1, u, False)
                    rest_z(end, NP - 1)
                    gate_attention(end)
                    add_attention(end)

        with ExitStack() as pb:
            def sbb(name, shape, dt=F32):
                return sb(name, shape, dt, pb)

            h2_hi = sbb("h2_hi", [P, S], F32R)
            h2_lo = sbb("h2_lo", [P, S], F32R)
            w1_hi = sbb("w1_hi", [P, E, H], F32R)
            w1_lo = sbb("w1_lo", [P, E, H], F32R)
            w2_hi = sbb("w2_hi", [P, E, HC, D], F32R)
            w2_lo = sbb("w2_lo", [P, E, HC, D], F32R)
            hidden = sbb("hidden", [P, 2, HC, S])
            hid_hi = sbb("hid_hi", [P, 2, HC, S], F32R)
            hid_lo = sbb("hid_lo", [P, 2, HC, S], F32R)
            w_raw = sbb("w_raw", [P, E, H])
            assert H == S and E == 2 * HC and HC * D == H
            logits = sbb("logits", [P, NT, E])
            top = sbb("top", [P, NT, E])
            chosen = sbb("chosen", [P, NT, E])
            shifted = sbb("shifted", [P, NT, E])
            expd = sbb("expd", [P, NT, E])
            kept = sbb("kept", [P, NT, E])
            w_now = sbb("w_now", [P, NT, E])
            w_sum = sbb("w_sum", [P, NT])
            w_rsum = sbb("w_rsum", [P, NT])
            w_T = sbb("w_T", [E, S])
            LO = 32
            w_split = sbb("w_split", [LO + E, S], F32R)
            pick_raw = sbb("pick_raw", [LO + E, E, P])
            pick = sbb("pick", [LO + E, E, P], F32R)
            w_row = sbb("w_row", [P, S])
            y_w = sbb("y_w", [P, S])
            acc = sbb("acc", [P, S])
            y_result = sbb("y_result", [P, NT, D])
            y_bank, w_bank = banks[:, 4, :], banks[:, 5, :]
            hT_bank, wT_bank, out_bank = banks[:, 6, :], banks[0:E, 6, :], banks[:, 6, :]
            logit_bank, b2_bank = banks[:, 7, 0:NT * E], banks[:, 7, :]

            def tile_of(x, b, t):
                return x[:, ds(b * NT + t, 1), :].rearrange("p a d -> p (a d)")

            def w_parts(layer, e):
                if layer == 1:
                    return w1_hi[:, e, :], w1_lo[:, e, :]
                return tuple(w[:, e, :, :].rearrange("p c d -> p (c d)") for w in (w2_hi, w2_lo))

            def raw_of(layer, e):
                return hidden[:, 1, e, :] if layer == 2 and e < HC else w_raw[:, e, :]

            def expert(b, e):
                return E * b + e

            load_w = [[sem(f"load_w{layer}_{e}") for e in range(E)] for layer in (1, 2)]
            w_hi_ok, w_split_ok, pick_made, pick_ok = sem("w_hi_ok"), sem("w_split_ok"), sem("pick_made"), sem("pick_ok")
            r_stat, r_mv, r_eps, r_rstd, r_xn = (sem(f"r_{n}") for n in ("stat", "mv", "eps", "rstd", "xn"))
            r_T_ps, r_full, r_hi, r_lo = (sem(f"r_{n}") for n in ("T_ps", "full", "hi", "lo"))
            r_logit_ps, r_shift, r_exp, r_w, r_wT_ps, r_wT, r_w_lo, r_b2_ps = (
                sem(f"r_{n}") for n in ("logit_ps", "shift", "exp", "w", "wT_ps", "wT", "w_lo", "b2_ps"))
            r_chain = sem("r_chain")
            hid_ps, hid, hid_hi_act, hid_hi_dve, hid_lo_ok = (
                sem(n) for n in ("hid_ps", "hid", "hid_hi_act", "hid_hi_dve", "hid_lo_ok"))
            w_ps, w_out, y_ps, y_weighted, y_summed, out_ps = (
                sem(n) for n in ("w_ps", "w_out", "y_ps", "y_weighted", "y_summed", "out_ps"))
            y_begun, y_out, stored = sem("y_begun"), sem("y_out"), sem("stored")

            with nc.Block() as block:
                @block.tensor
                def _(pe):
                    def norm_T(b):
                        pe.wait_ge(r_xn, NT * b + NT)
                        for t in range(NT):
                            mm = pe.transpose(hT_bank[:, t * P:(t + 1) * P], xn[:, t, :], ident[:, :])
                        mm.then_inc(r_T_ps, 1)

                    def router_logits(b):
                        pe.wait_ge(r_full, b + 1)
                        for t in range(NT):
                            mm = pe.matmul(logit_bank[:, t * E:(t + 1) * E], hf[:, t * P:(t + 1) * P],
                                           wr_sb[:, :], start=True, stop=True)
                        mm.then_inc(r_logit_ps, 1)

                    def weights_T(b):
                        pe.wait_ge(r_w, b + 1)
                        for t in range(NT):
                            mm = pe.matmul(wT_bank[:, t * P:(t + 1) * P], w_now[:, t, :], ident[:, :],
                                           start=True, stop=True)
                        mm.then_inc(r_wT_ps, 1)

                    def weigh_b2(b):
                        pe.wait_ge(r_wT, 2 * b + 2)
                        pe.matmul(b2_bank, b2_rows[:, :], w_T[:, :], start=True, stop=True).then_inc(r_b2_ps, 1)

                    def first_layer(b, e, begin):
                        if e == 0:
                            pe.wait_ge(r_lo, b + 1)
                        for c in range(HC):
                            if not begin:
                                pe.wait_ge(hid, HC * expert(b, e - 1) + c + 1)
                            cols = slice(c * P, (c + 1) * P)
                            pe.matmul(banks[:, c, :], w1_hi[:, e, cols], h2_hi[:, :], start=True, stop=False)
                            pe.matmul(banks[:, c, :], w1_lo[:, e, cols], h2_hi[:, :], start=False, stop=False)
                            pe.matmul(banks[:, c, :], w1_hi[:, e, cols], h2_lo[:, :], start=False, stop=True)\
                                .then_inc(hid_ps, 1)

                    def second_layer(b, e, begin):
                        if e == 0:
                            pe.wait_ge(r_w_lo, b + 1)
                        if not begin:
                            pe.wait_ge(w_out, expert(b, e))
                            pe.wait_ge(y_weighted, expert(b, e))
                        pe.matmul(w_bank, pick[:, e, :], w_split[:, :], start=True, stop=True).then_inc(w_ps, 1)
                        for c in range(HC):
                            pe.wait_ge(hid_lo_ok, HC * expert(b, e) + c + 1)
                            hi, lo = hid_hi[:, e % 2, c, :], hid_lo[:, e % 2, c, :]
                            pe.matmul(y_bank, w2_hi[:, e, c, :], hi, start=(c == 0), stop=False)
                            pe.matmul(y_bank, w2_lo[:, e, c, :], hi, start=False, stop=False)
                            mm = pe.matmul(y_bank, w2_hi[:, e, c, :], lo, start=False, stop=(c == HC - 1))
                        mm.then_inc(y_ps, 1)

                    def sum_T(b):
                        pe.wait_ge(y_summed, expert(b, E))
                        for t in range(NT):
                            mm = pe.transpose(out_bank[:, t * P:(t + 1) * P], acc[:, t * P:(t + 1) * P], ident[:, :])
                        mm.then_inc(out_ps, 1)

                    def body(b, first, last):
                        for e in range(E):
                            if first:
                                pe.wait_ge(w_split_ok, e + 1)
                            first_layer(b, e, first and e == 0)
                            if e == 0 and first:
                                weights_T(0)
                            if first and e > 0:
                                pe.wait_ge(w_split_ok, E + e)
                                if e == 1:
                                    pe.wait_ge(pick_ok, 2)
                            if e > 0:
                                second_layer(b, e - 1, first and e == 1)
                            elif not first:
                                second_layer(b - 1, E - 1, False)
                            if e == 1:
                                weigh_b2(b)
                                if not first:
                                    sum_T(b - 1)
                            if not last and e == 3:
                                norm_T(b + 1)
                            if not last and e == 5:
                                router_logits(b + 1)
                            if not last and e == 7:
                                weights_T(b + 1)
                            if first and e == E - 1:
                                pe.wait_ge(w_split_ok, 2 * E)

                    norm_T(0)
                    router_logits(0)
                    batches(pe, body)
                    second_layer(B - 1, E - 1, False)
                    sum_T(B - 1)

                @block.gpsimd
                def _(pool):
                    def inv_std(b):
                        wait_alone(pool, r_mv, NT * b + NT)
                        pool.tensor_scalar(var_eps[:, :], meanvar[:, :, 1], EPS, 1.0, ALU.add, ALU.mult).then_inc(r_eps, 1)
                        pool.wait_ge(r_eps, b + 1)
                        pool.tensor_tensor(rstd[:, :], var_eps[:, :], neg_half[:, :], ALU.pow).then_inc(r_rstd, 1)

                    def add_expert(b, e):
                        wait_alone(pool, y_weighted, expert(b, e) + 1)
                        if e == 0:
                            wait_alone(pool, y_begun, b + 1)
                        else:
                            wait_alone(pool, y_summed, expert(b, e))
                        pool.tensor_tensor(acc[:, :], acc[:, :], y_w[:, :], ALU.add).then_inc(y_summed, 1)

                    def body(b, first, last):
                        if not first:
                            add_expert(b - 1, E - 1)
                        add_expert(b, 0)
                        if not last:
                            inv_std(b + 1)
                        for e in range(1, E - 1):
                            add_expert(b, e)

                    inv_std(0)
                    pool.memset(pick_raw[:, :, :], 0.0).then_inc(pick_made, 1)
                    for i, base in enumerate((0, -LO)):
                        pool.wait_ge(pick_made, i + 1)
                        pool.affine_select(out=pick_raw[:, :, :], in_=pick_raw[:, :, :], compare_op=ALU.not_equal,
                                           fill=1.0, base=base, pattern=[[-1, E], [0, P]], channel_multiplier=1)\
                            .then_inc(pick_made, 1)
                    batches(pool, body)
                    add_expert(B - 1, E - 1)

                @block.scalar
                def _(act):
                    def h_evac(b):
                        act.wait_ge(r_T_ps, b + 1)
                        if not isinstance(b, int) or b > 0:
                            act.wait_ge(r_lo, b)
                        act.activation(hf[:, :], hT_bank, ACT.Identity, bias=mod_cols[:, 3, ds(b, 1)],
                                       scale=mod_cols[:, 4, ds(b, 1)]).then_inc(r_full, 1)

                    def logit_exp(b):
                        act.wait_ge(r_shift, b + 1)
                        act.activation(expd[:, :, :], shifted[:, :, :], ACT.Exp).then_inc(r_exp, 1)

                    def round_h(b):
                        act.wait_ge(r_full, b + 1)
                        if not isinstance(b, int) or b > 0:
                            act.wait_ge(hid_ps, HC * expert(b, 0))
                        act.activation(h2_hi[:, :], hf[:, :], ACT.Copy).then_inc(r_hi, 1)

                    def round_weights(b):
                        act.wait_ge(r_wT_ps, b + 1)
                        if not isinstance(b, int) or b > 0:
                            act.wait_ge(w_ps, expert(b, 0))
                        else:
                            act.wait_ge(pick_ok, 1)
                        act.activation(w_T[:, :], wT_bank, ACT.Copy).then_inc(r_wT, 1)
                        act.activation(w_split[0:E, :], wT_bank, ACT.Copy).then_inc(r_wT, 1)

                    def weights_out(b, e, begin):
                        act.wait_ge(w_ps, expert(b, e) + 1)
                        if not begin:
                            act.wait_ge(y_weighted, expert(b, e))
                        act.activation(w_row[:, :], w_bank, ACT.Copy).then_inc(w_out, 1)

                    def round_w(layer, e):
                        act.wait_ge(load_w[layer - 1][e], 16)
                        act.activation(w_parts(layer, e)[0], raw_of(layer, e), ACT.Copy).then_inc(w_hi_ok, 1)

                    def hidden_chunk(b, e, c, young):
                        act.wait_ge(hid_ps, HC * expert(b, e) + c + 1)
                        if not young:
                            act.wait_ge(hid_lo_ok, HC * expert(b, e - 2) + c + 1)
                        act.activation(hidden[:, e % 2, c, :], banks[:, c, :], ACT.Gelu,
                                       bias=b1_cols[:, e * HC + c:e * HC + c + 1]).then_inc(hid, 1)

                    def round_chunk(b, e, c, young):
                        act.wait_ge(hid, HC * expert(b, e) + c + 1)
                        if not young:
                            act.wait_ge(y_ps, expert(b, e - 1))
                        act.activation(hid_hi[:, e % 2, c, :], hidden[:, e % 2, c, :], ACT.Copy).then_inc(hid_hi_act, 1)

                    def body(b, first, last):
                        for e in range(E):
                            young = first and e < 2
                            if first and e == 1:
                                for other in range(HC):
                                    round_w(2, other)
                                act.wait_ge(w_split_ok, E + HC)
                            if first and HC <= e + 2 < E:
                                round_w(2, e + 2)
                            hidden_chunk(b, e, 0, young)
                            hidden_chunk(b, e, 1, young)
                            round_chunk(b, e, 0, young)
                            hidden_chunk(b, e, 2, young)
                            if e == 7 and not last:
                                round_h(b + 1)
                            round_chunk(b, e, 1, young)
                            hidden_chunk(b, e, 3, young)
                            if e > 0:
                                weights_out(b, e - 1, first and e == 1)
                            elif not first:
                                weights_out(b - 1, E - 1, False)
                            if e == 0:
                                round_weights(b)
                            if e == 4 and not last:
                                h_evac(b + 1)
                            if e == 6 and not last:
                                logit_exp(b + 1)

                    h_evac(0)
                    round_h(0)
                    for e in range(E):
                        round_w(1, e)
                    logit_exp(0)
                    batches(act, body)
                    weights_out(B - 1, E - 1, False)

                @block.vector
                def _(dve):
                    CHAIN = 5 + NT
                    links = [0]

                    def link(b, ins):
                        links[0] += 1
                        ins.then_inc(r_chain, 1)
                        wait_alone(dve, r_chain, CHAIN * b + links[0])

                    def norm_stats(b):
                        links[0] = 0
                        for t in range(NT):
                            dve.bn_stats(stats[:, t, :], tile_of(x_all, b, t)).then_inc(r_stat, 1)
                        for t in range(NT):
                            wait_alone(dve, r_stat, NT * b + t + 1)
                            dve.bn_aggr(meanvar[:, t, :], stats[:, t, :]).then_inc(r_mv, 1)

                    def norm_rows(b):
                        dve.wait_ge(r_rstd, b + 1)
                        for t in range(NT):
                            dve.tensor_scalar(xn[:, t, :], tile_of(x_all, b, t), meanvar[:, t, 0:1], rstd[:, t:t + 1],
                                              ALU.subtract, ALU.mult).then_inc(r_xn, 1)

                    def rest_h(b):
                        dve.wait_ge(r_hi, b + 1)
                        dve.tensor_tensor(h2_lo[:, :], hf[:, :], h2_hi[:, :].bitcast(F32), ALU.subtract)\
                            .then_inc(r_lo, 1)

                    def choose(b):
                        dve.wait_ge(r_logit_ps, b + 1)
                        link(b, dve.tensor_tensor(logits[:, :, :], logit_bank.rearrange("p (t e) -> p t e", t=NT),
                                                  br_b[:, :].unsqueeze(1).broadcast_to([P, NT, E]), ALU.add))
                        for t in range(NT):
                            link(b, dve.max(out=top[:, t, :], in_=logits[:, t, :]))
                        dve.tensor_tensor(shifted[:, :, :], logits[:, :, :],
                                          top[:, :, 0:1].broadcast_to([P, NT, E]), ALU.subtract).then_inc(r_shift, 1)
                        link(b, dve.tensor_tensor(chosen[:, :, :], logits[:, :, :],
                                                  top[:, :, 1:2].broadcast_to([P, NT, E]), ALU.is_ge))

                    def weights(b):
                        dve.wait_ge(r_exp, b + 1)
                        link(b, dve.tensor_tensor(kept[:, :, :], expd[:, :, :], chosen[:, :, :], ALU.mult))
                        link(b, dve.tensor_reduce(w_sum[:, :], kept[:, :, :], AX.X, ALU.add))
                        link(b, dve.reciprocal(w_rsum[:, :], w_sum[:, :]))
                        rsum = w_rsum[:, :].unsqueeze(2).broadcast_to([P, NT, E])
                        dve.tensor_tensor(w_now[:, :, :], kept[:, :, :], rsum, ALU.mult).then_inc(r_w, 1)
                        assert links[0] == CHAIN

                    def rest_weights(b):
                        dve.wait_ge(r_wT, 2 * b + 2)
                        dve.tensor_tensor(w_split[LO:LO + E, :], wT_bank, w_split[0:E, :].bitcast(F32), ALU.subtract)\
                            .then_inc(r_w_lo, 1)

                    def begin_sum(b, begin):
                        dve.wait_ge(r_b2_ps, b + 1)
                        if not begin:
                            dve.wait_ge(out_ps, b)
                        dve.tensor_scalar(acc[:, :], b2_bank, gate_cols[:, 1, ds(b, 1)], None, ALU.mult)\
                            .then_inc(y_begun, 1)

                    def split_w(i, layer, e):
                        hi, lo = w_parts(layer, e)
                        dve.wait_ge(w_hi_ok, i + 1)
                        dve.tensor_tensor(lo, raw_of(layer, e), hi.bitcast(F32), ALU.subtract).then_inc(w_split_ok, 1)

                    def rest_chunk(b, e, c, young):
                        hi, full = hid_hi[:, e % 2, c, :], hidden[:, e % 2, c, :]
                        if c < 2:
                            dve.wait_ge(hid_hi_act, 2 * expert(b, e) + c + 1)
                        else:
                            dve.wait_ge(hid, HC * expert(b, e) + c + 1)
                            if not young:
                                dve.wait_ge(y_ps, expert(b, e - 1))
                            dve.tensor_copy(hi, full).then_inc(hid_hi_dve, 1)
                            dve.wait_ge(hid_hi_dve, 2 * expert(b, e) + c - 1)
                        dve.tensor_tensor(hid_lo[:, e % 2, c, :], full, hi.bitcast(F32), ALU.subtract)\
                            .then_inc(hid_lo_ok, 1)

                    def weigh_expert(b, e, begin):
                        dve.wait_ge(w_out, expert(b, e) + 1)
                        dve.wait_ge(y_ps, expert(b, e) + 1)
                        if not begin:
                            dve.wait_ge(y_summed, expert(b, e))
                        dve.scalar_tensor_tensor(out=y_w[:, :], in0=y_bank, scalar=gate_cols[:, 1, ds(b, 1)],
                                                 in1=w_row[:, :], op0=ALU.mult, op1=ALU.mult).then_inc(y_weighted, 1)

                    def finish(b, begin):
                        dve.wait_ge(out_ps, b + 1)
                        if not begin:
                            dve.wait_ge(stored, 16 * b)
                        dve.tensor_tensor(y_result[:, :, :], out_bank.rearrange("p (t d) -> p t d", t=NT),
                                          x_all[:, ds(b * NT, NT), :], ALU.add).then_inc(y_out, 1)

                    def body(b, first, last):
                        for e in range(E):
                            young = first and e < 2
                            if first:
                                for other in (range(HC) if e == 1 else (e + 2,) if HC <= e + 2 < E else ()):
                                    split_w(E + other, 2, other)
                            for c in range(HC):
                                if e == 7 and c == 1 and not last:
                                    rest_h(b + 1)
                                rest_chunk(b, e, c, young)
                            if e == 0:
                                rest_weights(b)
                            if e > 0:
                                if e == 1:
                                    begin_sum(b, first)
                                weigh_expert(b, e - 1, first and e == 1)
                            elif not first:
                                weigh_expert(b - 1, E - 1, False)
                            if e == 1 and not first:
                                finish(b - 1, isinstance(b, int) and b == 1)
                            if not last and e == 1:
                                norm_stats(b + 1)
                            if not last and e == 2:
                                norm_rows(b + 1)
                            if not last and e == 5:
                                choose(b + 1)
                            if not last and e == 6:
                                weights(b + 1)

                    norm_stats(0)
                    dve.memset(w_split[:, :].bitcast(F32), 0.0).then_inc(pick_ok, 1)
                    norm_rows(0)
                    rest_h(0)
                    choose(0)
                    for e in range(E):
                        split_w(e, 1, e)
                    weights(0)
                    dve.wait_ge(pick_made, 3)
                    dve.tensor_copy(pick[:, :, :], pick_raw[:, :, :]).then_inc(pick_ok, 1)
                    batches(dve, body)
                    weigh_expert(B - 1, E - 1, False)
                    finish(B - 1, False)

                @block.sync
                def _(sp):
                    for e in range(E):
                        sp.dma_start(raw_of(1, e), W1[e]).then_inc(load_w[0][e], 16)
                    for e in range(E):
                        if e >= HC:
                            sp.wait_ge(w_split_ok, e + 1)
                        sp.dma_start(raw_of(2, e).rearrange("p (c d) -> p c d", c=HC),
                                     W2[e].rearrange("(c p) d -> p c d", p=P)).then_inc(load_w[1][e], 16)

                    def body(b, first, last):
                        sp.wait_ge(y_out, b + 1)
                        sp.dma_start(out[ds(b, 1)].rearrange("b (t p) d -> p (b t) d", p=P), y_result[:, :, :])\
                            .then_inc(stored, 16)

                    batches(sp, body)
                    sp.wait_ge(stored, 16 * B)


_INS = ["L0_attn_resid", "L0_attn_W_Q", "L0_attn_W_K", "L0_attn_W_V", "L0_attn_W_out", "L0_attn_b_out",
        "L0_ffn_W1", "L0_ffn_b1", "L0_ffn_W2", "L0_ffn_b2", "L0_ffn_Wr", "L0_ffn_br", "L0_c", "L0_wmod"]


def kernel(**inputs):
    import numpy as _np
    import concourse.bacc as _bacc
    from concourse import mybir as _mybir
    from concourse.bass_utils import run_bass_kernel_spmd as _run

    nc = _bacc.Bacc("TRN2", target_bir_lowering=False, num_devices=1)
    arrays, args = {}, []
    for name in _INS:
        a = _np.ascontiguousarray(inputs[name])
        arrays[f"in_{name}_dram"] = a
        args.append(nc.dram_tensor(f"in_{name}_dram", a.shape, _mybir.dt.from_np(a.dtype), kind="ExternalInput").ap())
    shape = inputs["L0_attn_resid"].shape
    args.append(nc.dram_tensor("out_0_dram", shape, _mybir.dt.from_np(_np.dtype("float32")), kind="ExternalOutput").ap())
    adaln_moe_kernel(nc, *args)
    r = _run(nc, [arrays], core_ids=[0])
    return r.results[0]["out_0_dram"]
```
